# Optimizing a Trainium2 kernel written in Bass

```python
import numpy as np
import jax
import jax.numpy as jnp

def _softmax(x, axis=-1):
    return jax.nn.softmax(x, axis=axis)

def _gelu(x):
    return jax.nn.gelu(x, approximate=True)

def _silu(x):
    return jax.nn.silu(x)

def _sigmoid(x):
    return jax.nn.sigmoid(x)

def _layernorm(x, axis=-1, eps=1e-05):
    m = jnp.mean(x, axis=axis, keepdims=True)
    v = jnp.var(x, axis=axis, keepdims=True)
    return (x - m) / jnp.sqrt(v + eps)

def _scatter_add(tgt, idx, src, axis=0):
    return tgt.at[idx].add(src)

def _segment_sum(src, seg, n):
    return jax.ops.segment_sum(src, seg, n)
kernel_name = 'mk_adj_resnorm_d2_adj_r2_696db3'

def setup_inputs(seed: int=0):
    np.random.seed(seed)
    _w = jnp.asarray

    def _rec_inputs():
        import jax
        import jax.numpy as jnp
        _gk = jax.random.key(seed)
        x = -0.0003929 + 0.9999 * jax.random.normal(jax.random.fold_in(_gk, 1), (128, 128, 256), jnp.float32)
        _w = (1.0 + jnp.arange(128, dtype=jnp.float32)) ** (-0.5)
        _w = _w / _w.mean()
        _pij = jnp.clip(0.125 * _w[:, None] * _w[None, :], 0.0, 1.0)
        _a = jax.random.uniform(jax.random.fold_in(_gk, 2), (128, 128)) < _pij
        _a = jnp.logical_or(_a, jnp.eye(128, dtype=bool))
        _af = _a.astype(jnp.float32)
        _af = _af * jax.random.uniform(jax.random.fold_in(_gk, 3), (128, 128), jnp.float32, 0.05, 1)
        adj = _af
        return (x, adj)
    x, adj = _rec_inputs()

    def _L0_gnn_setup():
        import jax, jax.numpy as jnp
        import numpy as np
        B, N, D, O = (8, 2048, 256, 256)
        key = jax.random.key(seed)
        k1, k2, k3, k4 = jax.random.split(key, 4)
        x = jax.random.normal(k1, (B, N, D), dtype=jnp.float32)
        adj = jax.random.uniform(k2, (N, N), dtype=jnp.float32)
        weight = jax.random.normal(k3, (D, O), dtype=jnp.float32) * 0.02
        bias = jax.random.normal(k4, (O,), dtype=jnp.float32) * 0.02
        return {'x': x, 'adj': adj, 'weight': weight, 'bias': bias}
    _L0_gnn_all = _L0_gnn_setup()
    _L0_gnn_in = {k: v for k, v in _L0_gnn_all.items() if k in ('weight', 'bias')}
    del _L0_gnn_all

    def _L1_gnn_setup():
        import jax, jax.numpy as jnp
        import numpy as np
        B, N, D, T = (64, 128, 256, 3)

        def _lin(v, W, b):
            return jnp.einsum('...i,oi->...o', v, W) + b
        key = jax.random.key(seed)
        ks = jax.random.split(key, 12)
        s2 = 1.0 / np.sqrt(2 * D)
        s1 = 1.0 / np.sqrt(D)
        return {'x': jax.random.normal(ks[0], (B, N, D), jnp.float32), 'in_mat': jax.random.uniform(ks[1], (N, N), jnp.float32) / N, 'out_mat': jax.random.uniform(ks[2], (N, N), jnp.float32) / N, 'w3_w': jax.random.normal(ks[3], (D, 2 * D), jnp.float32) * s2, 'w3_b': jnp.zeros((D,), jnp.float32), 'u3_w': jax.random.normal(ks[4], (D, D), jnp.float32) * s1, 'u3_b': jnp.zeros((D,), jnp.float32), 'w4_w': jax.random.normal(ks[5], (D, 2 * D), jnp.float32) * s2, 'w4_b': jnp.zeros((D,), jnp.float32), 'w5_w': jax.random.normal(ks[6], (D, 2 * D), jnp.float32) * s2, 'w5_b': jnp.zeros((D,), jnp.float32), 'u5_w': jax.random.normal(ks[7], (D, D), jnp.float32) * s1, 'u5_b': jnp.zeros((D,), jnp.float32)}
    _L1_gnn_all = _L1_gnn_setup()
    _L1_gnn_in = {k: v for k, v in _L1_gnn_all.items() if k in ('w3_w', 'w3_b', 'u3_w', 'u3_b', 'w4_w', 'w4_b', 'w5_w', 'w5_b', 'u5_w', 'u5_b')}
    del _L1_gnn_all
    return {'x': x, 'adj': adj, 'L0_gnn_weight': _L0_gnn_in['weight'], 'L0_gnn_bias': _L0_gnn_in['bias'], 'L1_gnn_w3_w': _L1_gnn_in['w3_w'], 'L1_gnn_w3_b': _L1_gnn_in['w3_b'], 'L1_gnn_u3_w': _L1_gnn_in['u3_w'], 'L1_gnn_u3_b': _L1_gnn_in['u3_b'], 'L1_gnn_w4_w': _L1_gnn_in['w4_w'], 'L1_gnn_w4_b': _L1_gnn_in['w4_b'], 'L1_gnn_w5_w': _L1_gnn_in['w5_w'], 'L1_gnn_w5_b': _L1_gnn_in['w5_b'], 'L1_gnn_u5_w': _L1_gnn_in['u5_w'], 'L1_gnn_u5_b': _L1_gnn_in['u5_b']}

def reference(x, adj, L0_gnn_weight, L0_gnn_bias, L1_gnn_w3_w, L1_gnn_w3_b, L1_gnn_u3_w, L1_gnn_u3_b, L1_gnn_w4_w, L1_gnn_w4_b, L1_gnn_w5_w, L1_gnn_w5_b, L1_gnn_u5_w, L1_gnn_u5_b):
    import jax
    import jax.numpy as jnp

    def _L0_gnn_ref(x, adj, weight, bias):
        import jax, jax.numpy as jnp
        import numpy as np
        B, N, D, O = (8, 2048, 256, 256)
        y = jnp.einsum('nm,bmd->bnd', adj, x)
        out = jnp.einsum('bnd,do->bno', y, weight) + bias
        return out

    def _L1_gnn_ref(x, in_mat, out_mat, w3_w, w3_b, u3_w, u3_b, w4_w, w4_b, w5_w, w5_b, u5_w, u5_b):
        import jax, jax.numpy as jnp
        import numpy as np
        B, N, D, T = (64, 128, 256, 3)

        def _lin(v, W, b):
            return jnp.einsum('...i,oi->...o', v, W) + b
        h = x
        for _ in range(T):
            a_in = jnp.einsum('nm,bmd->bnd', in_mat, h)
            a_out = jnp.einsum('nm,bmd->bnd', out_mat, h)
            av = jnp.concatenate([a_in, a_out], axis=-1)
            z = jax.nn.sigmoid(_lin(av, w3_w, w3_b) + _lin(h, u3_w, u3_b))
            r = jax.nn.sigmoid(_lin(av, w4_w, w4_b) + _lin(h, u3_w, u3_b))
            hv = jnp.tanh(_lin(av, w5_w, w5_b) + _lin(r * h, u5_w, u5_b))
            h = (1.0 - z) * h + z * hv
        return h
    x = _layernorm(x + _L0_gnn_ref(x, adj, L0_gnn_weight, L0_gnn_bias), axis=-1)
    x = _layernorm(x + _L1_gnn_ref(x, adj, adj, L1_gnn_w3_w, L1_gnn_w3_b, L1_gnn_u3_w, L1_gnn_u3_b, L1_gnn_w4_w, L1_gnn_w4_b, L1_gnn_w5_w, L1_gnn_w5_b, L1_gnn_u5_w, L1_gnn_u5_b), axis=-1)
    return x

_drawn_inputs = setup_inputs


def setup_inputs(seed=0):
    import zlib

    import numpy as np

    out = dict(_drawn_inputs(seed))
    spreads = {'L1_gnn_w3_b': (0.0, 0.281),
     'L1_gnn_u3_b': (0.0, 0.267),
     'L1_gnn_w4_b': (0.0, 2.0),
     'L1_gnn_w5_b': (0.0, 0.1),
     'L1_gnn_u5_b': (0.0, 0.1)}
    factors = {}
    for name, (base, spread) in spreads.items():
        noise = np.random.default_rng([zlib.crc32(name.encode()), seed]).standard_normal(out[name].shape)
        drawn = base * np.exp(spread * noise) if base else spread * noise
        out[name] = jnp.asarray(drawn.astype(out[name].dtype))
    for name, factor in factors.items():
        out[name] = (out[name] * factor).astype(out[name].dtype)
    return out
```

```python
from contextlib import ExitStack

import concourse.bass as bass
from concourse import mybir

F32 = mybir.dt.float32
F32R = mybir.dt.float32r
ALU = mybir.AluOpType
ACT = mybir.ActivationFunctionType

P = 128
G = 4
C = 2
STEPS = 3
SLOTS = 2 * STEPS
EPS = 1e-5


def gnn_kernel(nc, x, adj_t, w0, b0, w3_t, w4_t, w5_t, u3_t, u5_t, biases, out):
    B, N, D = x.shape
    assert N == P and D == C * P and B % (2 * G) == 0
    PAIRS = B // (2 * G)
    COLS = G * N

    x_groups = x.rearrange("(n b) m d -> n m b d", b=G)
    out_groups = out.rearrange("(n b) m d -> n m b d", b=G)

    with ExitStack() as ctx:
        def sb(name, shape, dt=F32):
            return ctx.enter_context(nc.sbuf_tensor(name, shape, dt))

        def sem(name):
            return ctx.enter_context(nc.semaphore(name))

        def two(make, name, *args):
            return [make(f"{name}_{g}", *args) for g in "ab"]

        adjt = sb("adjt", [P, N])
        ident = sb("ident", [P, P])
        bias_row = sb("bias_row", [P, D])
        bias_in = sb("bias_in", [P, 5, C])
        bias_z = sb("bias_z", [P, C])
        bias_r = sb("bias_r", [P, C])
        bias_h = sb("bias_h", [P, C])
        minus_half = sb("minus_half", [P, G])
        eps = sb("eps", [P, G])
        w0_raw = sb("w0_raw", [P, C, D])
        w_raw = [sb(f"w{n}_raw", [P, 2 * C, D]) for n in (3, 4, 5)]
        u_raw = [sb(f"u{n}_raw", [P, C, D]) for n in (3, 5)]
        w0_hi, w0_lo = sb("w0_hi", [P, C, D], F32R), sb("w0_lo", [P, C, D], F32R)
        gate_hi = {n: sb(f"{n}_hi", [P, C, D], F32R) for n in ("w3", "w4", "w5", "u3", "u5")}
        gate_lo = {n: sb(f"{n}_lo", [P, C, D], F32R) for n in ("w3", "w4", "w5", "u3", "u5")}

        gate_raw = {"u3": u_raw[0][:, :, :], "u5": u_raw[1][:, :, :],
                    "w3": w_raw[0][:, 0:C, :], "w4": w_raw[1][:, 0:C, :], "w5": w_raw[2][:, 0:C, :]}

        x_in = two(sb, "x_in", [P, G, D])
        x_bias = two(sb, "x_bias", [P, G, D])
        h0_nat = two(sb, "h0_nat", [P, G, D])
        h0_t = two(sb, "h0_t", [P, C, COLS])
        h_t = two(sb, "h_t", [P, C, COLS])
        h_hi, h_lo = two(sb, "h_hi", [P, C, COLS], F32R), two(sb, "h_lo", [P, C, COLS], F32R)
        a_hi, a_lo = two(sb, "a_hi", [P, C, COLS], F32R), two(sb, "a_lo", [P, C, COLS], F32R)
        result = two(sb, "result", [P, G, D])

        h_nat = sb("h_nat", [P, G, D])
        ax_hi, ax_lo = sb("ax_hi", [P, C, COLS], F32R), sb("ax_lo", [P, C, COLS], F32R)
        u_sb = sb("u_sb", [P, C, COLS])
        z_sb = sb("z_sb", [P, C, COLS])
        rh = sb("rh", [P, C, COLS])
        rh_hi, rh_lo = sb("rh_hi", [P, C, COLS], F32R), sb("rh_lo", [P, C, COLS], F32R)
        hv = sb("hv", [P, C, COLS])
        stats = sb("stats", [P, G, 6])
        meanvar = sb("meanvar", [P, G, 2])
        var_eps = sb("var_eps", [P, G])
        rstd = sb("rstd", [P, G])

        ps_r = ctx.enter_context(nc.psum_tensor("ps_r", [P, C, COLS], F32))
        ps_z = ctx.enter_context(nc.psum_tensor("ps_z", [P, C, COLS], F32))
        ps_h = ctx.enter_context(nc.psum_tensor("ps_h", [P, C, COLS], F32))
        ps_x = ctx.enter_context(nc.psum_tensor("ps_x", [P, C, COLS], F32))

        def by_node(ps):
            return ps[:, :, :].rearrange("p c (b d) -> p (c b) d", d=D)

        ps_x_nat = by_node(ps_x)

        adj_in, w0_in, gates_in, bias_in_s = sem("adj_in"), sem("w0_in"), sem("gates_in"), sem("bias_in_s")
        x_loaded = two(sem, "x_loaded")
        out_stored = two(sem, "out_stored")
        ident_zero, ident_ready = sem("ident_zero"), sem("ident_ready")
        w0_hi_ready, w0_ready = sem("w0_hi_ready"), sem("w0_ready")
        gate_sum, gates_hi_ready, gates_ready = sem("gate_sum"), sem("gates_hi_ready"), sem("gates_ready")
        biases_ready = sem("biases_ready")
        norm_constants = sem("norm_constants")
        u_done, z_done, r_done, h_done = sem("u_done"), sem("z_done"), sem("r_done"), sem("h_done")
        graph_done = sem("graph_done")
        step_t_done = sem("step_t_done")
        first_t_done, last_t_done = sem("first_t_done"), sem("last_t_done")
        ax_done, y_done = sem("ax_done"), sem("y_done")
        u_copied, z_ready, r_ready = sem("u_copied"), sem("z_ready"), sem("r_ready")
        rh_hi_ready, hv_ready, h_hi_ready = sem("rh_hi_ready"), sem("hv_ready"), sem("h_hi_ready")
        a_hi_ready, ax_hi_ready = sem("a_hi_ready"), sem("ax_hi_ready")
        h_nat_ready, h0_t_ready, result_copied = sem("h_nat_ready"), sem("h0_t_ready"), sem("result_copied")
        z_added, rh_ready, rh_lo_ready = sem("z_added"), sem("rh_ready"), sem("rh_lo_ready")
        diff_ready, scaled_ready = sem("diff_ready"), sem("scaled_ready")
        h_ready, h_lo_ready = sem("h_ready"), sem("h_lo_ready")
        last_h_ready = sem("last_h_ready")
        a_lo_ready, ax_lo_ready = sem("a_lo_ready"), sem("ax_lo_ready")
        y_added, h0_stats, h0_var, h0_ready = sem("y_added"), sem("h0_stats"), sem("h0_var"), sem("h0_ready")
        out_stats, out_var, out_ready = sem("out_stats"), sem("out_var"), sem("out_ready")
        x_biased = sem("x_biased")
        h0_var_eps, h0_rstd = sem("h0_var_eps"), sem("h0_rstd")
        out_var_eps, out_rstd = sem("out_var_eps"), sem("out_rstd")

        def slot_no(p, k):
            return p * SLOTS + k

        def group_no(p, g):
            return p * 2 + g

        def step_t_no(p, s, g):
            return p * 4 + 2 * (s - 1) + g

        def run_pairs(eng, pair):
            pair(0, True, PAIRS == 1)
            if PAIRS > 2:
                with eng.Fori(1, PAIRS - 1) as p:
                    pair(p, False, False)
            if PAIRS > 1:
                pair(PAIRS - 1, False, True)

        block = ctx.enter_context(nc.Block())

        @block.sync
        def _(sp):
            sp.dma_start(adjt[:, :], adj_t).then_inc(adj_in, 16)
            sp.dma_start(x_in[0][:, :, :], x_groups[0]).then_inc(x_loaded[0], 16)
            sp.dma_start(w0_raw[:, :, :], w0.rearrange("(c p) o -> p c o", p=P)).then_inc(w0_in, 16)
            sp.dma_start(bias_row[:, :], b0.to_broadcast([P, D])).then_inc(bias_in_s, 16)
            sp.dma_start(x_in[1][:, :, :], x_groups[1]).then_inc(x_loaded[1], 16)
            sp.dma_start(u_raw[0][:, :, :], u3_t.rearrange("(c p) o -> p c o", p=P)).then_inc(gates_in, 16)
            for raw, w in zip(w_raw, (w3_t, w4_t, w5_t)):
                sp.dma_start(raw[:, :, :], w.rearrange("(c p) o -> p c o", p=P)).then_inc(gates_in, 16)
            sp.dma_start(u_raw[1][:, :, :], u5_t.rearrange("(c p) o -> p c o", p=P)).then_inc(gates_in, 16)
            sp.dma_start(bias_in[:, :, :], biases).then_inc(gates_in, 16)

            def pair(p, first, last):
                if not last:
                    for g in range(2):
                        sp.wait_ge(ax_done, group_no(p, g) + 1)
                        sp.wait_ge(x_biased, group_no(p, g) + 1)
                        sp.dma_start(x_in[g][:, :, :], x_groups[group_no(p + 1, g)]).then_inc(x_loaded[g], 16)
                if not first:
                    for g in range(2):
                        sp.wait_ge(out_ready, group_no(p - 1, g) + 1)
                        sp.dma_start(out_groups[group_no(p - 1, g)], result[g][:, :, :]).then_inc(out_stored[g], 16)

            run_pairs(sp, pair)
            for g in range(2):
                sp.wait_ge(out_ready, group_no(PAIRS - 1, g) + 1)
                sp.dma_start(out_groups[group_no(PAIRS - 1, g)], result[g][:, :, :]).then_inc(out_stored[g], 16)
            for g in range(2):
                sp.wait_ge(out_stored[g], 16 * PAIRS)

        @block.tensor
        def _(pe):
            def split_product(psum, name, hi, lo, start, stop, signal=None, hi_wait=None, lo_wait=None):
                w_hi, w_lo = gate_hi[name], gate_lo[name]
                for o in range(C):
                    rows = slice(o * P, (o + 1) * P)
                    for c in range(C):
                        if hi_wait is not None and o == 0:
                            hi_wait(c)
                        pe.matmul(psum[:, o, :], w_hi[:, c, rows], hi[:, c, :], start=start and c == 0, stop=False,
                                  skip_group_check=True)
                        if lo_wait is not None and o == 0:
                            lo_wait(c)
                        pe.matmul(psum[:, o, :], w_hi[:, c, rows], lo[:, c, :], start=False, stop=False,
                                  skip_group_check=True)
                    for c in range(C):
                        mm = pe.matmul(psum[:, o, :], w_lo[:, c, rows], hi[:, c, :], start=False,
                                       stop=stop and c == C - 1, skip_group_check=True)
                    if signal is not None:
                        mm.then_inc(signal, 1)

            def graph(psum, nat, signal):
                for c in range(C):
                    for b in range(G):
                        mm = pe.matmul(psum[:, c, b * N:(b + 1) * N], nat[:, b, c * P:(c + 1) * P], adjt[:, :],
                                       start=True, stop=True)
                mm.then_inc(signal, 1)

            def to_nodes(src, signal):
                for b in range(G):
                    for c in range(C):
                        mm = pe.transpose(ps_x_nat[:, b, c * P:(c + 1) * P], src[:, c, b * N:(b + 1) * N], ident[:, :])
                mm.then_inc(signal, 1)

            def to_features(src, signal):
                for c in range(C):
                    for b in range(G):
                        mm = pe.transpose(ps_x[:, c, b * N:(b + 1) * N], src[:, b, c * P:(c + 1) * P], ident[:, :])
                mm.then_inc(signal, 1)

            def first_graph(psum, p, g):
                pe.wait_ge(x_loaded[g], (p + 1) * 16)
                graph(psum, x_in[g], ax_done)

            def first_weights(psum, hi, lo, p, g):
                pe.wait_ge(ax_lo_ready, group_no(p, g) + 1)
                for b in range(G):
                    for c in range(C):
                        cols = slice(b * N, (b + 1) * N)
                        for n, (v, w) in enumerate(((hi, w0_hi), (hi, w0_lo), (lo, w0_hi))):
                            mm = pe.matmul(by_node(psum)[:, b, :], v[:, c, cols], w[:, c, :],
                                           start=n == 0 and c == 0, stop=n == 2 and c == C - 1,
                                           skip_group_check=True)
                mm.then_inc(y_done, 1)

            pe.wait_ge(adj_in, 16)
            first_graph(ps_x, 0, 0)
            first_graph(ps_z, 0, 1)
            pe.wait_ge(w0_ready, 1)
            first_weights(ps_r, ax_hi, ax_lo, 0, 0)
            first_weights(ps_h, a_hi[1], a_lo[1], 0, 1)
            pe.wait_ge(ident_ready, 1)
            pe.wait_ge(h0_ready, 1)
            to_features(h0_nat[0], first_t_done)
            pe.wait_ge(h0_t_ready, 1)
            graph(ps_x, h0_nat[0], graph_done)

            def slot(p, k, first, last):
                s, g = divmod(k, 2)
                i = slot_no(p, k)
                begin = first and k == 0
                has_next = not (last and k == SLOTS - 1)
                other = 1 - g
                if not last and k in (1, 3):
                    pe.wait_ge(a_lo_ready, i + 1)
                    first_graph(ps_x, p + 1, k // 2)
                if not last and k in (2, 4):
                    pe.wait_ge(a_lo_ready, i + 1)
                    first_weights(ps_x, ax_hi, ax_lo, p + 1, k // 2 - 1)

                pe.wait_ge(h_lo_ready, i + 1)
                if not begin:
                    pe.wait_ge(r_ready, 2 * i)
                if begin:
                    pe.wait_ge(gates_ready, 1)
                split_product(ps_r, "u3", h_hi[g], h_lo[g], True, True, u_done)

                if k == 0 or (k == SLOTS - 1 and not last):
                    q = p if k == 0 else p + 1
                    pe.wait_ge(h0_ready, group_no(q, other) + 1)
                    pe.wait_ge(a_lo_ready, i + 1)
                    to_features(h0_nat[other], first_t_done)

                pe.wait_ge(a_lo_ready, i + 1)
                if not begin:
                    pe.wait_ge(z_added, i)
                if begin:
                    pe.wait_ge(gates_ready, 2)
                split_product(ps_z, "w3", a_hi[g], a_lo[g], True, True, z_done)

                if 1 <= k <= SLOTS - 2:
                    pe.wait_ge(h_ready, 2 * i)
                    if not last and k in (1, 3):
                        pe.wait_ge(ax_lo_ready, group_no(p + 1, k // 2) + 1)
                    elif not last and k in (2, 4):
                        pe.wait_ge(y_added, group_no(p + 1, k // 2 - 1) + 1)
                    to_nodes(h_t[other], step_t_done)
                elif not begin:
                    q = p - 1 if k == 0 else p
                    pe.wait_ge(last_h_ready, group_no(q, other) + 1)
                    if k == 0:
                        pe.wait_ge(h0_t_ready, group_no(p, 1) + 1)
                    elif not last:
                        pe.wait_ge(h0_t_ready, group_no(p + 1, 0) + 1)
                    to_nodes(h_t[other], last_t_done)

                pe.wait_ge(u_copied, i + 1)
                if begin:
                    pe.wait_ge(gates_ready, 3)
                split_product(ps_r, "w4", a_hi[g], a_lo[g], False, True, r_done)

                if 1 <= k <= SLOTS - 2:
                    pe.wait_ge(h_nat_ready, step_t_no(p, (k + 1) // 2, other) + 1)
                    graph(ps_x, h_nat, graph_done)
                elif k == 0:
                    if begin:
                        pe.wait_ge(h0_t_ready, 2)
                    else:
                        pe.wait_ge(result_copied, group_no(p - 1, 1) + 1)
                    graph(ps_x, h0_nat[1], graph_done)
                elif not last:
                    pe.wait_ge(result_copied, group_no(p, 0) + 1)
                    graph(ps_x, h0_nat[0], graph_done)

                if not begin:
                    pe.wait_ge(hv_ready, 2 * i)
                if begin:
                    pe.wait_ge(gates_ready, 4)
                split_product(ps_h, "w5", a_hi[g], a_lo[g], True, False)

                def rh_hi_there(c):
                    pe.wait_ge(rh_hi_ready, 2 * i + c + 1)

                def rh_lo_there(c):
                    pe.wait_ge(rh_lo_ready, 2 * i + c + 1)

                if begin:
                    pe.wait_ge(gates_ready, 5)
                split_product(ps_h, "u5", rh_hi, rh_lo, False, True, h_done, rh_hi_there, rh_lo_there)

            def pair(p, first, last):
                for k in range(SLOTS):
                    slot(p, k, first, last)

            run_pairs(pe, pair)
            pe.wait_ge(last_h_ready, 2 * PAIRS)
            pe.wait_ge(result_copied, 2 * PAIRS - 1)
            to_nodes(h_t[1], last_t_done)


        @block.scalar
        def _(act):
            def copy(dst, src):
                return act.activation(dst, src, ACT.Copy)

            act.wait_ge(w0_in, 16)
            copy(w0_hi[:, :, :], w0_raw[:, :, :]).then_inc(w0_hi_ready, 1)

            def first_graph_parts(psum, hi, p, g):
                act.wait_ge(ax_done, group_no(p, g) + 1)
                copy(hi[:, :, :], psum[:, :, :]).then_inc(ax_hi_ready, 1)

            def first_state(p, g):
                act.wait_ge(first_t_done, group_no(p, g) + 1)
                copy(h0_t[g][:, :, :], ps_x[:, :, :]).then_inc(h0_t_ready, 1)
                act.wait_ge(h0_t_ready, group_no(p, g) + 1)
                copy(h_hi[g][:, :, :], h0_t[g][:, :, :]).then_inc(h_hi_ready, 1)

            def graph_parts(i, g):
                act.wait_ge(graph_done, i + 1)
                copy(a_hi[g][:, :, :], ps_x[:, :, :]).then_inc(a_hi_ready, 1)

            def candidate(i):
                for c in range(C):
                    act.wait_ge(h_done, 2 * i + c + 1)
                    act.activation(hv[:, c, :], ps_h[:, c, :], ACT.Tanh, bias=bias_h[:, c:c + 1]).then_inc(hv_ready, 1)

            def take_result(p, g):
                act.wait_ge(last_t_done, group_no(p, g) + 1)
                if not (isinstance(p, int) and p == 0):
                    act.wait_ge(out_stored[g], p * 16)
                copy(result[g][:, :, :], ps_x_nat).then_inc(result_copied, 1)

            first_graph_parts(ps_x, ax_hi, 0, 0)
            first_graph_parts(ps_z, a_hi[1], 0, 1)
            act.wait_ge(gate_sum, 3)
            for n, name in enumerate(("u3", "w3", "w4", "w5", "u5")):
                copy(gate_hi[name][:, :, :], gate_raw[name]).then_inc(gates_hi_ready, 1)
            first_state(0, 0)
            graph_parts(0, 0)

            def slot(p, k, first, last):
                s, g = divmod(k, 2)
                i = slot_no(p, k)
                begin = first and k == 0
                other = 1 - g
                if begin:
                    act.wait_ge(biases_ready, 1)
                else:
                    candidate(i - 1)
                if not last and k in (1, 3):
                    first_graph_parts(ps_x, ax_hi, p + 1, k // 2)
                if 1 <= k <= SLOTS - 2:
                    act.wait_ge(h_ready, 2 * i)
                    copy(h_hi[other][:, :, :], h_t[other][:, :, :]).then_inc(h_hi_ready, 1)
                act.wait_ge(u_done, 2 * i + 2)
                copy(u_sb[:, :, :], ps_r[:, :, :]).then_inc(u_copied, 1)
                if 1 <= k <= SLOTS - 2:
                    act.wait_ge(step_t_done, step_t_no(p, (k + 1) // 2, other) + 1)
                    copy(h_nat[:, :, :], ps_x_nat).then_inc(h_nat_ready, 1)
                elif k == 0:
                    if not begin:
                        act.wait_ge(last_h_ready, group_no(p - 1, 1) + 1)
                    first_state(p, 1)
                    if not begin:
                        take_result(p - 1, 1)
                else:
                    if not last:
                        act.wait_ge(last_h_ready, group_no(p, 0) + 1)
                        first_state(p + 1, 0)
                    take_result(p, 0)
                for c in range(C):
                    act.wait_ge(r_done, 2 * i + c + 1)
                    act.activation(rh[:, c, :], ps_r[:, c, :], ACT.Sigmoid, bias=bias_r[:, c:c + 1]).then_inc(r_ready, 1)
                    act.wait_ge(rh_ready, 2 * i + c + 1)
                    copy(rh_hi[:, c, :], rh[:, c, :]).then_inc(rh_hi_ready, 1)
                if not (last and k == SLOTS - 1):
                    graph_parts(i + 1, other)
                act.wait_ge(z_added, i + 1)
                for c in range(C):
                    z = act.activation(z_sb[:, c, :], z_sb[:, c, :], ACT.Sigmoid, bias=bias_z[:, c:c + 1])
                z.then_inc(z_ready, 1)

            def pair(p, first, last):
                for k in range(SLOTS):
                    slot(p, k, first, last)

            run_pairs(act, pair)
            candidate(slot_no(PAIRS - 1, SLOTS - 1))
            take_result(PAIRS - 1, 1)

        @block.vector
        def _(dve):
            def low_part(dst, full, hi):
                return dve.tensor_tensor(dst, full, hi.bitcast(F32), ALU.subtract)

            def first_graph_parts(psum, hi, lo, p, g):
                dve.wait_ge(ax_hi_ready, group_no(p, g) + 1)
                low_part(lo[:, :, :], psum[:, :, :], hi[:, :, :]).then_inc(ax_lo_ready, 1)

            def row_statistics(rows, measured):
                for b in range(G):
                    st = dve.bn_stats(stats[:, b, :], rows[:, b, :])
                st.then_inc(measured, 1)

            def mean_and_variance(ready):
                for b in range(G):
                    mv = dve.bn_aggr(meanvar[:, b, :], stats[:, b, :])
                mv.then_inc(ready, 1)

            def normalise(rows, ready):
                for b in range(G):
                    ts = dve.tensor_scalar(rows[:, b, :], rows[:, b, :], meanvar[:, b, 0:1], rstd[:, b:b + 1],
                                           ALU.subtract, ALU.mult)
                ts.then_inc(ready, 1)

            def first_sum(psum, p, g):
                dve.wait_ge(y_done, group_no(p, g) + 1)
                dve.wait_ge(x_biased, group_no(p, g) + 1)
                dve.tensor_tensor(h0_nat[g][:, :, :], by_node(psum), x_bias[g][:, :, :], ALU.add).then_inc(y_added, 1)
                dve.wait_ge(y_added, group_no(p, g) + 1)
                row_statistics(h0_nat[g], h0_stats)

            def first_norm(p, g):
                dve.wait_ge(h0_rstd, group_no(p, g) + 1)
                normalise(h0_nat[g], h0_ready)

            def result_statistics(p, g):
                dve.wait_ge(result_copied, group_no(p, g) + 1)
                row_statistics(result[g], out_stats)

            def result_norm(p, g):
                dve.wait_ge(out_rstd, group_no(p, g) + 1)
                normalise(result[g], out_ready)

            def first_state_parts(i, p, g):
                dve.wait_ge(h_hi_ready, i + 1)
                dve.wait_ge(h0_t_ready, group_no(p, g) + 1)
                low_part(h_lo[g][:, :, :], h0_t[g][:, :, :], h_hi[g][:, :, :]).then_inc(h_lo_ready, 1)

            def graph_parts(i, g):
                dve.wait_ge(a_hi_ready, i + 1)
                low_part(a_lo[g][:, :, :], ps_x[:, :, :], a_hi[g][:, :, :]).then_inc(a_lo_ready, 1)

            def state_update(i, s, g):
                before = h0_t[g] if s == 0 else h_t[g]
                for c in range(C):
                    dve.wait_ge(hv_ready, 2 * i + c + 1)
                    dve.tensor_tensor(hv[:, c, :], hv[:, c, :], before[:, c, :], ALU.subtract).then_inc(diff_ready, 1)
                    dve.wait_ge(diff_ready, 2 * i + c + 1)
                    if c == 0:
                        dve.wait_ge(z_ready, i + 1)
                    dve.tensor_tensor(hv[:, c, :], hv[:, c, :], z_sb[:, c, :], ALU.mult).then_inc(scaled_ready, 1)
                    dve.wait_ge(scaled_ready, 2 * i + c + 1)
                    dve.tensor_tensor(h_t[g][:, c, :], hv[:, c, :], before[:, c, :], ALU.add).then_inc(h_ready, 1)

            def add_residual(i, g):
                dve.wait_ge(h_ready, 2 * i + 2)
                dve.tensor_tensor(h_t[g][:, :, :], h_t[g][:, :, :], h0_t[g][:, :, :], ALU.add).then_inc(last_h_ready, 1)

            dve.wait_ge(w0_hi_ready, 1)
            low_part(w0_lo[:, :, :], w0_raw[:, :, :], w0_hi[:, :, :]).then_inc(w0_ready, 1)
            first_graph_parts(ps_x, ax_hi, ax_lo, 0, 0)
            first_graph_parts(ps_z, a_hi[1], a_lo[1], 0, 1)
            dve.wait_ge(gates_in, 16 * 6)
            for raw in w_raw:
                dve.tensor_tensor(raw[:, 0:C, :], raw[:, 0:C, :], raw[:, C:2 * C, :], ALU.add).then_inc(gate_sum, 1)
            dve.tensor_tensor(bias_z[:, :], bias_in[:, 0, :], bias_in[:, 3, :], ALU.add)
            dve.tensor_tensor(bias_r[:, :], bias_in[:, 1, :], bias_in[:, 3, :], ALU.add)
            dve.tensor_tensor(bias_h[:, :], bias_in[:, 2, :], bias_in[:, 4, :], ALU.add).then_inc(biases_ready, 1)

            def gate_low_parts(names, at):
                for n, name in enumerate(names):
                    dve.wait_ge(gates_hi_ready, at + n + 1)
                    low_part(gate_lo[name][:, :, :], gate_raw[name], gate_hi[name][:, :, :]).then_inc(gates_ready, 1)

            first_sum(ps_r, 0, 0)
            dve.wait_ge(h0_stats, 1)
            mean_and_variance(h0_var)
            gate_low_parts(("u3", "w3"), 0)
            first_norm(0, 0)
            first_sum(ps_h, 0, 1)
            gate_low_parts(("w4", "w5"), 2)
            first_state_parts(0, 0, 0)
            dve.wait_ge(h0_stats, 2)
            mean_and_variance(h0_var)
            gate_low_parts(("u5",), 4)
            first_norm(0, 1)
            graph_parts(0, 0)

            def slot(p, k, first, last):
                s, g = divmod(k, 2)
                i = slot_no(p, k)
                begin = first and k == 0
                other = 1 - g
                if not begin:
                    state_update(i - 1, (s - 1 if g == 0 else s) % STEPS, other)
                if k == 0 and not begin:
                    add_residual(i - 1, 1)
                if k == SLOTS - 1:
                    add_residual(i - 1, 0)
                if k == 0 and not first:
                    result_norm(p - 1, 0)
                if k == 1 and not first:
                    result_norm(p - 1, 1)
                if k == 0:
                    first_state_parts(i + 1, p, 1)
                if k == SLOTS - 1 and not last:
                    first_state_parts(i + 1, p + 1, 0)
                if not last and k in (1, 3):
                    first_graph_parts(ps_x, ax_hi, ax_lo, p + 1, k // 2)
                if not last and k in (2, 4):
                    first_sum(ps_x, p + 1, k // 2 - 1)
                if 1 <= k <= SLOTS - 2:
                    dve.wait_ge(h_hi_ready, i + 2)
                    low_part(h_lo[other][:, :, :], h_t[other][:, :, :], h_hi[other][:, :, :]).then_inc(h_lo_ready, 1)
                dve.wait_ge(u_copied, i + 1)
                dve.wait_ge(z_done, 2 * i + 2)
                if not last and k in (2, 4):
                    dve.wait_ge(h0_stats, group_no(p + 1, k // 2 - 1) + 1)
                dve.tensor_tensor(z_sb[:, :, :], ps_z[:, :, :], u_sb[:, :, :], ALU.add).then_inc(z_added, 1)
                if not last and k in (2, 4):
                    mean_and_variance(h0_var)
                before = h0_t[g] if s == 0 else h_t[g]
                for c in range(C):
                    dve.wait_ge(r_ready, 2 * i + c + 1)
                    dve.tensor_tensor(rh[:, c, :], rh[:, c, :], before[:, c, :], ALU.mult).then_inc(rh_ready, 1)
                    dve.wait_ge(rh_hi_ready, 2 * i + c + 1)
                    low_part(rh_lo[:, c, :], rh[:, c, :], rh_hi[:, c, :]).then_inc(rh_lo_ready, 1)
                if k == 0 and not first:
                    result_statistics(p - 1, 1)
                    dve.wait_ge(out_stats, group_no(p - 1, 1) + 1)
                if k == SLOTS - 1:
                    result_statistics(p, 0)
                    dve.wait_ge(out_stats, group_no(p, 0) + 1)
                if not (last and k == SLOTS - 1):
                    graph_parts(i + 1, other)
                if (k == 0 and not first) or k == SLOTS - 1:
                    mean_and_variance(out_var)
                if not last and k in (2, 4):
                    first_norm(p + 1, k // 2 - 1)

            def pair(p, first, last):
                for k in range(SLOTS):
                    slot(p, k, first, last)

            run_pairs(dve, pair)
            end = slot_no(PAIRS - 1, SLOTS - 1)
            state_update(end, STEPS - 1, 1)
            add_residual(end, 1)
            result_norm(PAIRS - 1, 0)
            result_statistics(PAIRS - 1, 1)
            dve.wait_ge(out_stats, 2 * PAIRS)
            mean_and_variance(out_var)
            result_norm(PAIRS - 1, 1)

        @block.gpsimd
        def _(pool):
            pool.memset(ident[:, :], 0.0).then_inc(ident_zero, 1)
            pool.memset(minus_half[:, :], -0.5)
            pool.memset(eps[:, :], EPS).then_inc(norm_constants, 1)
            pool.wait_ge(ident_zero, 1)
            pool.affine_select(out=ident[:, :], in_=ident[:, :], compare_op=ALU.not_equal, fill=1.0, base=0,
                               pattern=[[-1, P]], channel_multiplier=1).then_inc(ident_ready, 1)
            pool.wait_ge(norm_constants, 1)

            def add_bias(p, g):
                pool.wait_ge(x_loaded[g], (p + 1) * 16)
                if isinstance(p, int) and p == 0:
                    pool.wait_ge(bias_in_s, 16)
                else:
                    pool.wait_ge(y_added, group_no(p - 1, g) + 1)
                pool.tensor_tensor(x_bias[g][:, :, :], x_in[g][:, :, :],
                                   bias_row[:, :].unsqueeze(1).to_broadcast([P, G, D]), ALU.add).then_inc(x_biased, 1)

            def inverse_deviation(var_ready, eps_added, rstd_ready, p, g):
                pool.wait_ge(var_ready, group_no(p, g) + 1)
                pool.tensor_tensor(var_eps[:, :], meanvar[:, :, 1], eps[:, :], ALU.add).then_inc(eps_added, 1)
                pool.wait_ge(eps_added, group_no(p, g) + 1)
                pool.tensor_tensor(rstd[:, :], var_eps[:, :], minus_half[:, :], ALU.pow).then_inc(rstd_ready, 1)

            for g in range(2):
                add_bias(0, g)
            for g in range(2):
                inverse_deviation(h0_var, h0_var_eps, h0_rstd, 0, g)

            def pair(p, first, last):
                if not first:
                    inverse_deviation(out_var, out_var_eps, out_rstd, p - 1, 1)
                if not last:
                    for g in range(2):
                        add_bias(p + 1, g)
                        inverse_deviation(h0_var, h0_var_eps, h0_rstd, p + 1, g)
                inverse_deviation(out_var, out_var_eps, out_rstd, p, 0)

            run_pairs(pool, pair)
            inverse_deviation(out_var, out_var_eps, out_rstd, PAIRS - 1, 1)


def kernel(x, adj, L0_gnn_weight, L0_gnn_bias, L1_gnn_w3_w, L1_gnn_w3_b, L1_gnn_u3_w, L1_gnn_u3_b, L1_gnn_w4_w,
           L1_gnn_w4_b, L1_gnn_w5_w, L1_gnn_w5_b, L1_gnn_u5_w, L1_gnn_u5_b):
    import numpy as np
    import concourse.bacc as bacc
    from concourse.bass_utils import run_bass_kernel_spmd

    def t(a):
        return np.ascontiguousarray(np.asarray(a).T)

    biases = np.stack([np.asarray(b) for b in (L1_gnn_w3_b, L1_gnn_w4_b, L1_gnn_w5_b, L1_gnn_u3_b, L1_gnn_u5_b)])
    arrays = {
        "x": np.ascontiguousarray(x),
        "adj_t": t(adj),
        "w0": np.ascontiguousarray(L0_gnn_weight),
        "b0": np.ascontiguousarray(L0_gnn_bias).reshape(1, -1),
        "w3_t": t(L1_gnn_w3_w),
        "w4_t": t(L1_gnn_w4_w),
        "w5_t": t(L1_gnn_w5_w),
        "u3_t": t(L1_gnn_u3_w),
        "u5_t": t(L1_gnn_u5_w),
        "biases": np.ascontiguousarray(biases.reshape(5, C, P).transpose(2, 0, 1)),
    }
    nc = bacc.Bacc("TRN2", target_bir_lowering=False, num_devices=1)
    args = [nc.dram_tensor(n, a.shape, mybir.dt.from_np(a.dtype), kind="ExternalInput").ap() for n, a in arrays.items()]
    out = nc.dram_tensor("out", arrays["x"].shape, F32, kind="ExternalOutput").ap()
    gnn_kernel(nc, *args, out)
    r = run_bass_kernel_spmd(nc, [arrays], core_ids=[0])
    return r.results[0]["out"]
```

```python
from contextlib import ExitStack

import concourse.bass as bass
from concourse import mybir

F32 = mybir.dt.float32
F32R = mybir.dt.float32r
ALU = mybir.AluOpType
ACT = mybir.ActivationFunctionType

P = 128
G = 4
C = 2
STEPS = 3
SLOTS = 2 * STEPS
EPS = 1e-5


def gnn_kernel(nc, x, adj_t, w0, b0, w3_t, w4_t, w5_t, u3_t, u5_t, biases, out):
    B, N, D = x.shape
    assert N == P and D == C * P and B % (2 * G) == 0
    PAIRS = B // (2 * G)
    COLS = G * N
    Q = 32
    BLOCKS = P // Q
    MOVED = 16 * BLOCKS * BLOCKS

    x_groups = x.rearrange("(n b) m d -> n m b d", b=G)
    out_groups = out.rearrange("(n b) m d -> n m b d", b=G)

    with ExitStack() as ctx:
        def sb(name, shape, dt=F32):
            return ctx.enter_context(nc.sbuf_tensor(name, shape, dt))

        def sem(name):
            return ctx.enter_context(nc.semaphore(name))

        def two(make, name, *args):
            return [make(f"{name}_{g}", *args) for g in "ab"]

        adjt = sb("adjt", [P, N])
        ident = sb("ident", [P, P])
        bias_row = sb("bias_row", [P, D])
        bias_in = sb("bias_in", [P, 5, C])
        bias_z = sb("bias_z", [P, C])
        bias_r = sb("bias_r", [P, C])
        bias_h = sb("bias_h", [P, C])
        minus_half = sb("minus_half", [P, G])
        eps = sb("eps", [P, G])
        w0_raw = sb("w0_raw", [P, C, D])
        w_raw = [sb(f"w{n}_raw", [P, 2 * C, D]) for n in (3, 4, 5)]
        u_raw = [sb(f"u{n}_raw", [P, C, D]) for n in (3, 5)]
        w0_hi, w0_lo = sb("w0_hi", [P, C, D], F32R), sb("w0_lo", [P, C, D], F32R)
        gate_hi = {n: sb(f"{n}_hi", [P, C, D], F32R) for n in ("w3", "w4", "w5", "u3", "u5")}
        gate_lo = {n: sb(f"{n}_lo", [P, C, D], F32R) for n in ("w3", "w4", "w5", "u3", "u5")}

        gate_raw = {"u3": u_raw[0][:, :, :], "u5": u_raw[1][:, :, :],
                    "w3": w_raw[0][:, 0:C, :], "w4": w_raw[1][:, 0:C, :], "w5": w_raw[2][:, 0:C, :]}

        x_in = two(sb, "x_in", [P, G, D])
        x_bias = two(sb, "x_bias", [P, G, D])
        h0_nat = two(sb, "h0_nat", [P, G, D])
        h0_t = two(sb, "h0_t", [P, C, COLS])
        h_t = two(sb, "h_t", [P, C, COLS])
        h_hi, h_lo = two(sb, "h_hi", [P, C, COLS], F32R), two(sb, "h_lo", [P, C, COLS], F32R)
        a_hi, a_lo = two(sb, "a_hi", [P, C, COLS], F32R), two(sb, "a_lo", [P, C, COLS], F32R)
        result = two(sb, "result", [P, G, D])

        h0_blocks = sb("h0_blocks", [P, BLOCKS, G * C, Q])
        h0_moved_in = two(sb, "h0_moved_in", [P, BLOCKS, G * C, Q])
        last_blocks = sb("last_blocks", [P, BLOCKS, C * G, Q])
        last_moved_in = two(sb, "last_moved_in", [P, BLOCKS, C * G, Q])

        h_nat = sb("h_nat", [P, G, D])
        ax_hi, ax_lo = sb("ax_hi", [P, C, COLS], F32R), sb("ax_lo", [P, C, COLS], F32R)
        u_sb = sb("u_sb", [P, C, COLS])
        z_sb = sb("z_sb", [P, C, COLS])
        rh = sb("rh", [P, C, COLS])
        rh_hi, rh_lo = sb("rh_hi", [P, C, COLS], F32R), sb("rh_lo", [P, C, COLS], F32R)
        hv = sb("hv", [P, C, COLS])

        def norm_buffers(name):
            return (sb(name + "_sums", [P, G, 6]), sb(name + "_meanvar", [P, G, 2]),
                    sb(name + "_var_eps_sb", [P, G]), sb(name + "_rstd_sb", [P, G]))

        h0_norm, out_norm = norm_buffers("h0"), norm_buffers("out")

        ps_r = ctx.enter_context(nc.psum_tensor("ps_r", [P, C, COLS], F32))
        ps_z = ctx.enter_context(nc.psum_tensor("ps_z", [P, C, COLS], F32))
        ps_h = ctx.enter_context(nc.psum_tensor("ps_h", [P, C, COLS], F32))
        ps_x = ctx.enter_context(nc.psum_tensor("ps_x", [P, C, COLS], F32))

        def by_node(ps):
            return ps[:, :, :].rearrange("p c (b d) -> p (c b) d", d=D)

        ps_x_nat = by_node(ps_x)

        adj_in, w0_in, gates_in, bias_in_s = sem("adj_in"), sem("w0_in"), sem("gates_in"), sem("bias_in_s")
        x_loaded = two(sem, "x_loaded")
        out_stored = two(sem, "out_stored")
        h0_moved, last_moved = two(sem, "h0_moved"), two(sem, "last_moved")
        ident_zero, ident_ready = sem("ident_zero"), sem("ident_ready")
        w0_hi_ready, w0_ready = sem("w0_hi_ready"), sem("w0_ready")
        gate_sum, gates_hi_ready, gates_ready = sem("gate_sum"), sem("gates_hi_ready"), sem("gates_ready")
        biases_ready = sem("biases_ready")
        norm_constants = sem("norm_constants")
        u_done, z_done, r_done, h_done = sem("u_done"), sem("z_done"), sem("r_done"), sem("h_done")
        graph_done = sem("graph_done")
        step_t_done = sem("step_t_done")
        first_t_done, last_t_done = sem("first_t_done"), sem("last_t_done")
        ax_done, y_done = sem("ax_done"), sem("y_done")
        u_copied, z_ready, r_ready = sem("u_copied"), sem("z_ready"), sem("r_ready")
        rh_hi_ready, hv_ready, h_hi_ready = sem("rh_hi_ready"), sem("hv_ready"), sem("h_hi_ready")
        a_hi_ready, ax_hi_ready = sem("a_hi_ready"), sem("ax_hi_ready")
        h_nat_ready, h0_t_ready = sem("h_nat_ready"), sem("h0_t_ready")
        z_added, rh_ready, rh_lo_ready = sem("z_added"), sem("rh_ready"), sem("rh_lo_ready")
        diff_ready, scaled_ready = sem("diff_ready"), sem("scaled_ready")
        h_ready, h_lo_ready = sem("h_ready"), sem("h_lo_ready")
        last_h_ready = sem("last_h_ready")
        h0_blocks_ready, last_blocks_ready = sem("h0_blocks_ready"), sem("last_blocks_ready")
        a_lo_ready, ax_lo_ready = sem("a_lo_ready"), sem("ax_lo_ready")
        y_added, h0_stats, h0_var, h0_ready = sem("y_added"), sem("h0_stats"), sem("h0_var"), sem("h0_ready")
        out_stats, out_var, out_ready = sem("out_stats"), sem("out_var"), sem("out_ready")
        last_sum_ready = sem("last_sum_ready")
        x_biased = sem("x_biased")
        h0_var_eps, h0_rstd = sem("h0_var_eps"), sem("h0_rstd")
        out_var_eps, out_rstd = sem("out_var_eps"), sem("out_rstd")

        def slot_no(p, k):
            return p * SLOTS + k

        def group_no(p, g):
            return p * 2 + g

        def step_t_no(p, s, g):
            return p * 4 + 2 * (s - 1) + g

        def run_pairs(eng, pair):
            pair(0, True, PAIRS == 1)
            if PAIRS > 2:
                with eng.Fori(1, PAIRS - 1) as p:
                    pair(p, False, False)
            if PAIRS > 1:
                pair(PAIRS - 1, False, True)

        block = ctx.enter_context(nc.Block())

        @block.sync
        def _(sp):
            sp.dma_start(adjt[:, :], adj_t).then_inc(adj_in, 16)
            sp.dma_start(x_in[0][:, :, :], x_groups[0]).then_inc(x_loaded[0], 16)
            sp.dma_start(w0_raw[:, :, :], w0.rearrange("(c p) o -> p c o", p=P)).then_inc(w0_in, 16)
            sp.dma_start(bias_row[:, :], b0.to_broadcast([P, D])).then_inc(bias_in_s, 16)
            sp.dma_start(x_in[1][:, :, :], x_groups[1]).then_inc(x_loaded[1], 16)
            sp.dma_start(u_raw[0][:, :, :], u3_t.rearrange("(c p) o -> p c o", p=P)).then_inc(gates_in, 16)
            for raw, w in zip(w_raw, (w3_t, w4_t, w5_t)):
                sp.dma_start(raw[:, :, :], w.rearrange("(c p) o -> p c o", p=P)).then_inc(gates_in, 16)
            sp.dma_start(u_raw[1][:, :, :], u5_t.rearrange("(c p) o -> p c o", p=P)).then_inc(gates_in, 16)
            sp.dma_start(bias_in[:, :, :], biases).then_inc(gates_in, 16)

            def move_blocks(blocks, moved_in, moved):
                for to in range(BLOCKS):
                    for fro in range(BLOCKS):
                        sp.dma_start(moved_in[to * Q:(to + 1) * Q, fro, :, :],
                                     blocks[fro * Q:(fro + 1) * Q, to, :, :]).then_inc(moved, 16)

            def move_h0(p, g):
                sp.wait_ge(h0_blocks_ready, group_no(p - 1, g) + 1)
                sp.wait_ge(h0_t_ready, group_no(p - 1, g) + 1)
                move_blocks(h0_blocks, h0_moved_in[g], h0_moved[g])

            def move_last(p, g):
                sp.wait_ge(last_blocks_ready, group_no(p, g) + 1)
                if not (isinstance(p, int) and p == 0):
                    sp.wait_ge(out_ready, group_no(p - 1, g) + 1)
                move_blocks(last_blocks, last_moved_in[g], last_moved[g])

            def store(p, g):
                sp.wait_ge(out_ready, group_no(p, g) + 1)
                sp.dma_start(out_groups[group_no(p, g)], result[g][:, :, :]).then_inc(out_stored[g], 16)

            def pair(p, first, last):
                if not last:
                    for g in range(2):
                        sp.wait_ge(ax_done, group_no(p, g) + 1)
                        sp.wait_ge(x_biased, group_no(p, g) + 1)
                        sp.dma_start(x_in[g][:, :, :], x_groups[group_no(p + 1, g)]).then_inc(x_loaded[g], 16)
                if not first:
                    move_last(p - 1, 1)
                    store(p - 1, 0)
                    store(p - 1, 1)
                if not last:
                    move_h0(p + 1, 0)
                    move_h0(p + 1, 1)
                    move_last(p, 0)

            run_pairs(sp, pair)
            store(PAIRS - 1, 0)
            for half in range(2):
                rows = slice(half * G // 2, (half + 1) * G // 2)
                sp.wait_ge(out_ready, 2 * PAIRS - 1 + half + 1)
                sp.dma_start(out_groups[2 * PAIRS - 1][:, rows, :], result[1][:, rows, :]).then_inc(out_stored[1], 16)
            sp.wait_ge(out_stored[0], 16 * PAIRS)
            sp.wait_ge(out_stored[1], 16 * (PAIRS + 1))

        @block.tensor
        def _(pe):
            def split_product(psum, name, hi, lo, start, stop, signal=None, hi_wait=None, lo_wait=None):
                w_hi, w_lo = gate_hi[name], gate_lo[name]
                for o in range(C):
                    rows = slice(o * P, (o + 1) * P)
                    for c in range(C):
                        if hi_wait is not None and o == 0:
                            hi_wait(c)
                        pe.matmul(psum[:, o, :], w_hi[:, c, rows], hi[:, c, :], start=start and c == 0, stop=False,
                                  skip_group_check=True)
                        if lo_wait is not None and o == 0:
                            lo_wait(c)
                        pe.matmul(psum[:, o, :], w_hi[:, c, rows], lo[:, c, :], start=False, stop=False,
                                  skip_group_check=True)
                    for c in range(C):
                        mm = pe.matmul(psum[:, o, :], w_lo[:, c, rows], hi[:, c, :], start=False,
                                       stop=stop and c == C - 1, skip_group_check=True)
                    if signal is not None:
                        mm.then_inc(signal, 1)

            def graph(psum, nat, signal):
                for c in range(C):
                    for b in range(G):
                        mm = pe.matmul(psum[:, c, b * N:(b + 1) * N], nat[:, b, c * P:(c + 1) * P], adjt[:, :],
                                       start=True, stop=True)
                mm.then_inc(signal, 1)

            def to_nodes(psum, src, signal, chunk_wait=None):
                for c in range(C):
                    if chunk_wait is not None:
                        chunk_wait(c)
                    for b in range(G):
                        mm = pe.transpose(by_node(psum)[:, b, c * P:(c + 1) * P], src[:, c, b * N:(b + 1) * N],
                                          ident[:, :])
                mm.then_inc(signal, 1)

            def to_features(psum, src, signal):
                for c in range(C):
                    for b in range(G):
                        mm = pe.transpose(psum[:, c, b * N:(b + 1) * N], src[:, b, c * P:(c + 1) * P], ident[:, :])
                mm.then_inc(signal, 1)

            def first_graph(psum, p, g):
                pe.wait_ge(x_loaded[g], (p + 1) * 16)
                graph(psum, x_in[g], ax_done)

            def first_weights(psum, hi, lo, p, g):
                pe.wait_ge(ax_lo_ready, group_no(p, g) + 1)
                for b in range(G):
                    for c in range(C):
                        cols = slice(b * N, (b + 1) * N)
                        for n, (v, w) in enumerate(((hi, w0_hi), (hi, w0_lo), (lo, w0_hi))):
                            mm = pe.matmul(by_node(psum)[:, b, :], v[:, c, cols], w[:, c, :],
                                           start=n == 0 and c == 0, stop=n == 2 and c == C - 1,
                                           skip_group_check=True)
                mm.then_inc(y_done, 1)

            pe.wait_ge(adj_in, 16)
            first_graph(ps_x, 0, 0)
            first_graph(ps_z, 0, 1)
            pe.wait_ge(w0_ready, 1)
            first_weights(ps_r, ax_hi, ax_lo, 0, 0)
            first_weights(ps_h, a_hi[1], a_lo[1], 0, 1)
            pe.wait_ge(ident_ready, 1)
            pe.wait_ge(h0_ready, 1)
            to_features(ps_z, h0_nat[0], first_t_done)
            graph(ps_x, h0_nat[0], graph_done)

            def slot(p, k, first, last):
                s, g = divmod(k, 2)
                i = slot_no(p, k)
                begin = first and k == 0
                has_next = not (last and k == SLOTS - 1)
                other = 1 - g
                if not last and k in (1, 3):
                    pe.wait_ge(a_lo_ready, i + 1)
                    first_graph(ps_x, p + 1, k // 2)
                if not last and k in (2, 4):
                    pe.wait_ge(a_lo_ready, i + 1)
                    first_weights(ps_x, ax_hi, ax_lo, p + 1, k // 2 - 1)

                pe.wait_ge(h_lo_ready, i + 1)
                if not begin:
                    pe.wait_ge(r_ready, 2 * i)
                if begin:
                    pe.wait_ge(gates_ready, 1)
                split_product(ps_r, "u3", h_hi[g], h_lo[g], True, True, u_done)

                if begin:
                    pe.wait_ge(h0_ready, 2)
                    pe.wait_ge(a_lo_ready, 1)
                    to_features(ps_x, h0_nat[1], first_t_done)

                pe.wait_ge(a_lo_ready, i + 1)
                if not begin:
                    pe.wait_ge(z_added, i)
                if begin:
                    pe.wait_ge(gates_ready, 2)
                split_product(ps_z, "w3", a_hi[g], a_lo[g], True, True, z_done)

                if 1 <= k <= SLOTS - 2:
                    pe.wait_ge(h_ready, 2 * i)
                    if not last and k in (1, 3):
                        pe.wait_ge(ax_lo_ready, group_no(p + 1, k // 2) + 1)
                    elif not last and k in (2, 4):
                        pe.wait_ge(y_added, group_no(p + 1, k // 2 - 1) + 1)
                    to_nodes(ps_x, h_t[other], step_t_done)

                pe.wait_ge(u_copied, i + 1)
                if begin:
                    pe.wait_ge(gates_ready, 3)
                split_product(ps_r, "w4", a_hi[g], a_lo[g], False, True, r_done)

                if 1 <= k <= SLOTS - 2:
                    pe.wait_ge(h_nat_ready, step_t_no(p, (k + 1) // 2, other) + 1)
                    graph(ps_x, h_nat, graph_done)
                elif not (last and k == SLOTS - 1):
                    if begin:
                        pe.wait_ge(h0_t_ready, 2)
                    pe.wait_ge(h0_ready, group_no(p if k == 0 else p + 1, other) + 1)
                    graph(ps_x, h0_nat[other], graph_done)
                else:
                    pe.wait_ge(last_h_ready, 2 * PAIRS - 1)
                    to_nodes(ps_x, h_t[0], last_t_done)

                if not begin:
                    pe.wait_ge(hv_ready, 2 * i)
                if begin:
                    pe.wait_ge(gates_ready, 4)
                split_product(ps_h, "w5", a_hi[g], a_lo[g], True, False)

                def rh_hi_there(c):
                    pe.wait_ge(rh_hi_ready, 2 * i + c + 1)

                def rh_lo_there(c):
                    pe.wait_ge(rh_lo_ready, 2 * i + c + 1)

                if begin:
                    pe.wait_ge(gates_ready, 5)
                split_product(ps_h, "u5", rh_hi, rh_lo, False, True, h_done, rh_hi_there, rh_lo_there)

            def pair(p, first, last):
                for k in range(SLOTS):
                    slot(p, k, first, last)

            run_pairs(pe, pair)

            def last_state_there(c):
                pe.wait_ge(last_h_ready, 2 * PAIRS - 1 + c + 1)

            to_nodes(ps_z, h_t[1], last_t_done, last_state_there)


        @block.scalar
        def _(act):
            def copy(dst, src):
                return act.activation(dst, src, ACT.Copy)

            act.wait_ge(w0_in, 16)
            copy(w0_hi[:, :, :], w0_raw[:, :, :]).then_inc(w0_hi_ready, 1)

            def first_graph_parts(psum, hi, p, g):
                act.wait_ge(ax_done, group_no(p, g) + 1)
                copy(hi[:, :, :], psum[:, :, :]).then_inc(ax_hi_ready, 1)

            def first_state(p, g):
                if isinstance(p, int) and p == 0:
                    act.wait_ge(first_t_done, g + 1)
                    copy(h0_t[g][:, :, :], (ps_z, ps_x)[g][:, :, :]).then_inc(h0_t_ready, 1)
                else:
                    act.wait_ge(h0_moved[g], p * MOVED)
                    for c in range(C):
                        cp = copy(h0_t[g][:, c, :].rearrange("p (b i e) -> p b i e", b=G, e=Q),
                                  h0_moved_in[g][:, :, :, :].rearrange("p i (b c) e -> p c b i e", c=C)[:, c])
                    cp.then_inc(h0_t_ready, 1)
                act.wait_ge(h0_t_ready, group_no(p, g) + 1)
                copy(h_hi[g][:, :, :], h0_t[g][:, :, :]).then_inc(h_hi_ready, 1)

            def graph_parts(i, g):
                act.wait_ge(graph_done, i + 1)
                copy(a_hi[g][:, :, :], ps_x[:, :, :]).then_inc(a_hi_ready, 1)

            def candidate(i):
                for c in range(C):
                    act.wait_ge(h_done, 2 * i + c + 1)
                    act.activation(hv[:, c, :], ps_h[:, c, :], ACT.Tanh, bias=bias_h[:, c:c + 1]).then_inc(hv_ready, 1)

            first_graph_parts(ps_x, ax_hi, 0, 0)
            first_graph_parts(ps_z, a_hi[1], 0, 1)
            act.wait_ge(gate_sum, 3)
            for n, name in enumerate(("u3", "w3", "w4", "w5", "u5")):
                copy(gate_hi[name][:, :, :], gate_raw[name]).then_inc(gates_hi_ready, 1)
            first_state(0, 0)
            graph_parts(0, 0)

            def slot(p, k, first, last):
                s, g = divmod(k, 2)
                i = slot_no(p, k)
                begin = first and k == 0
                other = 1 - g
                if begin:
                    act.wait_ge(biases_ready, 1)
                else:
                    candidate(i - 1)
                if not last and k in (1, 3):
                    first_graph_parts(ps_x, ax_hi, p + 1, k // 2)
                if 1 <= k <= SLOTS - 2:
                    act.wait_ge(h_ready, 2 * i)
                    copy(h_hi[other][:, :, :], h_t[other][:, :, :]).then_inc(h_hi_ready, 1)
                act.wait_ge(u_done, 2 * i + 2)
                copy(u_sb[:, :, :], ps_r[:, :, :]).then_inc(u_copied, 1)
                if 1 <= k <= SLOTS - 2:
                    act.wait_ge(step_t_done, step_t_no(p, (k + 1) // 2, other) + 1)
                    copy(h_nat[:, :, :], ps_x_nat).then_inc(h_nat_ready, 1)
                elif k == 0:
                    if not begin:
                        act.wait_ge(last_h_ready, group_no(p - 1, 1) + 1)
                    first_state(p, 1)
                elif not last:
                    act.wait_ge(last_h_ready, group_no(p, 0) + 1)
                    first_state(p + 1, 0)
                for c in range(C):
                    act.wait_ge(r_done, 2 * i + c + 1)
                    act.activation(rh[:, c, :], ps_r[:, c, :], ACT.Sigmoid, bias=bias_r[:, c:c + 1]).then_inc(r_ready, 1)
                for c in range(C):
                    act.wait_ge(rh_ready, 2 * i + c + 1)
                    copy(rh_hi[:, c, :], rh[:, c, :]).then_inc(rh_hi_ready, 1)
                if not (last and k == SLOTS - 1):
                    graph_parts(i + 1, other)
                act.wait_ge(z_added, i + 1)
                for c in range(C):
                    z = act.activation(z_sb[:, c, :], z_sb[:, c, :], ACT.Sigmoid, bias=bias_z[:, c:c + 1])
                z.then_inc(z_ready, 1)

            def pair(p, first, last):
                for k in range(SLOTS):
                    slot(p, k, first, last)

            run_pairs(act, pair)
            candidate(slot_no(PAIRS - 1, SLOTS - 1))

        @block.vector
        def _(dve):
            def low_part(dst, full, hi):
                return dve.tensor_tensor(dst, full, hi.bitcast(F32), ALU.subtract)

            def first_graph_parts(psum, hi, lo, p, g):
                dve.wait_ge(ax_hi_ready, group_no(p, g) + 1)
                low_part(lo[:, :, :], psum[:, :, :], hi[:, :, :]).then_inc(ax_lo_ready, 1)

            def row_statistics(norm, rows, measured):
                sums = norm[0]
                for b in range(G):
                    st = dve.bn_stats(sums[:, b, :], rows(b))
                st.then_inc(measured, 1)

            def mean_and_variance(norm, ready):
                sums, meanvar = norm[0], norm[1]
                for b in range(G):
                    mv = dve.bn_aggr(meanvar[:, b, :], sums[:, b, :])
                mv.then_inc(ready, 1)

            def normalise(norm, dst, rows, ready, batches=range(G)):
                meanvar, rstd = norm[1], norm[3]
                for b in batches:
                    ts = dve.tensor_scalar(dst(b), rows(b), meanvar[:, b, 0:1], rstd[:, b:b + 1],
                                           ALU.subtract, ALU.mult)
                ts.then_inc(ready, 1)

            def rows_of(tensor):
                return lambda b: tensor[:, b, :]

            def first_sum(psum, p, g):
                dve.wait_ge(y_done, group_no(p, g) + 1)
                dve.wait_ge(x_biased, group_no(p, g) + 1)
                dve.tensor_tensor(h0_nat[g][:, :, :], by_node(psum), x_bias[g][:, :, :], ALU.add).then_inc(y_added, 1)
                dve.wait_ge(y_added, group_no(p, g) + 1)
                row_statistics(h0_norm, rows_of(h0_nat[g]), h0_stats)

            def first_norm(p, g):
                dve.wait_ge(h0_rstd, group_no(p, g) + 1)
                normalise(h0_norm, rows_of(h0_nat[g]), rows_of(h0_nat[g]), h0_ready)

            def first_blocks(p, g):
                if g == 1:
                    dve.wait_ge(h0_moved[0], p * MOVED)
                elif not (isinstance(p, int) and p == 1):
                    dve.wait_ge(h0_moved[1], (p - 1) * MOVED)
                dve.wait_ge(h0_ready, group_no(p, g) + 1)
                dve.transpose(h0_blocks[:, :, :, :].rearrange("p j m e -> p m j e"),
                              h0_nat[g][:, :, :].rearrange("p b (c j e) -> p (b c) j e", c=C, e=Q)
                              ).then_inc(h0_blocks_ready, 1)

            def last_state_blocks(p, g):
                if g == 1:
                    dve.wait_ge(last_moved[0], (p + 1) * MOVED)
                elif not (isinstance(p, int) and p == 0):
                    dve.wait_ge(last_moved[1], p * MOVED)
                dve.wait_ge(last_h_ready, group_no(p, g) + 1)
                dve.transpose(last_blocks[:, :, :, :].rearrange("p j m e -> p m j e"),
                              h_t[g][:, :, :].rearrange("p c (b j e) -> p (c b) j e", b=G, e=Q)
                              ).then_inc(last_blocks_ready, 1)

            def last_rows(g):
                return lambda b: last_moved_in[g][:, :, :, :].rearrange("p i (c b) e -> p b c i e", b=G)[:, b]

            def result_rows(g):
                return lambda b: result[g][:, b, :].rearrange("p (c i e) -> p c i e", c=C, e=Q)

            def result_statistics(p, g):
                dve.wait_ge(last_moved[g], (p + 1) * MOVED)
                row_statistics(out_norm, last_rows(g), out_stats)

            def result_norm(p, g):
                if not (isinstance(p, int) and p == 0):
                    dve.wait_ge(out_stored[g], p * 16)
                dve.wait_ge(out_rstd, group_no(p, g) + 1)
                normalise(out_norm, result_rows(g), last_rows(g), out_ready)

            def first_state_parts(i, p, g):
                dve.wait_ge(h_hi_ready, i + 1)
                dve.wait_ge(h0_t_ready, group_no(p, g) + 1)
                low_part(h_lo[g][:, :, :], h0_t[g][:, :, :], h_hi[g][:, :, :]).then_inc(h_lo_ready, 1)

            def graph_parts(i, g):
                dve.wait_ge(a_hi_ready, i + 1)
                low_part(a_lo[g][:, :, :], ps_x[:, :, :], a_hi[g][:, :, :]).then_inc(a_lo_ready, 1)

            def state_update(i, s, g, added=None, ready=h_ready):
                before = h0_t[g] if s == 0 else h_t[g]
                added = before if added is None else added
                for c in range(C):
                    dve.wait_ge(hv_ready, 2 * i + c + 1)
                    dve.tensor_tensor(hv[:, c, :], hv[:, c, :], before[:, c, :], ALU.subtract).then_inc(diff_ready, 1)
                    dve.wait_ge(diff_ready, 2 * i + c + 1)
                    if c == 0:
                        dve.wait_ge(z_ready, i + 1)
                    dve.tensor_tensor(hv[:, c, :], hv[:, c, :], z_sb[:, c, :], ALU.mult).then_inc(scaled_ready, 1)
                    dve.wait_ge(scaled_ready, 2 * i + c + 1)
                    dve.tensor_tensor(h_t[g][:, c, :], hv[:, c, :], added[:, c, :], ALU.add).then_inc(ready, 1)

            def add_residual(i, g):
                dve.wait_ge(h_ready, 2 * i + 2)
                dve.tensor_tensor(h_t[g][:, :, :], h_t[g][:, :, :], h0_t[g][:, :, :], ALU.add).then_inc(last_h_ready, 1)

            dve.wait_ge(w0_hi_ready, 1)
            low_part(w0_lo[:, :, :], w0_raw[:, :, :], w0_hi[:, :, :]).then_inc(w0_ready, 1)
            first_graph_parts(ps_x, ax_hi, ax_lo, 0, 0)
            first_graph_parts(ps_z, a_hi[1], a_lo[1], 0, 1)
            first_sum(ps_r, 0, 0)
            dve.wait_ge(h0_stats, 1)
            mean_and_variance(h0_norm, h0_var)
            dve.wait_ge(gates_in, 16 * 6)
            for raw in w_raw:
                dve.tensor_tensor(raw[:, 0:C, :], raw[:, 0:C, :], raw[:, C:2 * C, :], ALU.add).then_inc(gate_sum, 1)
            dve.tensor_tensor(bias_z[:, :], bias_in[:, 0, :], bias_in[:, 3, :], ALU.add)
            dve.tensor_tensor(bias_r[:, :], bias_in[:, 1, :], bias_in[:, 3, :], ALU.add)
            dve.tensor_tensor(bias_h[:, :], bias_in[:, 2, :], bias_in[:, 4, :], ALU.add).then_inc(biases_ready, 1)
            first_norm(0, 0)
            first_sum(ps_h, 0, 1)
            dve.wait_ge(h0_stats, 2)
            mean_and_variance(h0_norm, h0_var)

            def gate_low_part(n, name):
                dve.wait_ge(gates_hi_ready, n + 1)
                low_part(gate_lo[name][:, :, :], gate_raw[name], gate_hi[name][:, :, :]).then_inc(gates_ready, 1)

            gate_low_part(0, "u3")
            first_state_parts(0, 0, 0)
            gate_low_part(1, "w3")
            graph_parts(0, 0)
            gate_low_part(2, "w4")
            first_norm(0, 1)
            gate_low_part(3, "w5")
            gate_low_part(4, "u5")

            def slot(p, k, first, last):
                s, g = divmod(k, 2)
                i = slot_no(p, k)
                begin = first and k == 0
                other = 1 - g
                if k in (1, 2) and not first:
                    dve.wait_ge(out_stats, group_no(p - 1, k - 1) + 1)
                if not begin:
                    state_update(i - 1, (s - 1 if g == 0 else s) % STEPS, other)
                if k in (1, 2) and not first:
                    mean_and_variance(out_norm, out_var)
                if k == 0 and not begin:
                    add_residual(i - 1, 1)
                if k == SLOTS - 1:
                    add_residual(i - 1, 0)
                if not last and k in (1, 3):
                    first_graph_parts(ps_x, ax_hi, ax_lo, p + 1, k // 2)
                if not last and k in (2, 4):
                    first_sum(ps_x, p + 1, k // 2 - 1)
                if 1 <= k <= SLOTS - 2:
                    dve.wait_ge(h_hi_ready, i + 2)
                    low_part(h_lo[other][:, :, :], h_t[other][:, :, :], h_hi[other][:, :, :]).then_inc(h_lo_ready, 1)
                dve.wait_ge(u_copied, i + 1)
                dve.wait_ge(z_done, 2 * i + 2)
                if not last and k in (2, 4):
                    dve.wait_ge(h0_stats, group_no(p + 1, k // 2 - 1) + 1)
                dve.tensor_tensor(z_sb[:, :, :], ps_z[:, :, :], u_sb[:, :, :], ALU.add).then_inc(z_added, 1)
                if not last and k in (2, 4):
                    mean_and_variance(h0_norm, h0_var)
                before = h0_t[g] if s == 0 else h_t[g]
                for c in range(C):
                    dve.wait_ge(r_ready, 2 * i + c + 1)
                    dve.tensor_tensor(rh[:, c, :], rh[:, c, :], before[:, c, :], ALU.mult).then_inc(rh_ready, 1)
                for c in range(C):
                    dve.wait_ge(rh_hi_ready, 2 * i + c + 1)
                    low_part(rh_lo[:, c, :], rh[:, c, :], rh_hi[:, c, :]).then_inc(rh_lo_ready, 1)
                if k == 0:
                    first_state_parts(i + 1, p, 1)
                if k == SLOTS - 1 and not last:
                    first_state_parts(i + 1, p + 1, 0)
                if not (last and k == SLOTS - 1):
                    graph_parts(i + 1, other)
                if k in (0, 1) and not first:
                    result_statistics(p - 1, k)
                if k in (1, 2) and not first:
                    result_norm(p - 1, k - 1)
                if not last and k in (2, 4):
                    first_norm(p + 1, k // 2 - 1)
                    first_blocks(p + 1, k // 2 - 1)
                if k == 0 and not begin:
                    last_state_blocks(p - 1, 1)
                if k == SLOTS - 1 and not last:
                    last_state_blocks(p, 0)

            def pair(p, first, last):
                for k in range(SLOTS):
                    slot(p, k, first, last)

            run_pairs(dve, pair)
            end = slot_no(PAIRS - 1, SLOTS - 1)
            dve.tensor_tensor(h0_t[1][:, :, :], h0_t[1][:, :, :], h_t[1][:, :, :], ALU.add).then_inc(last_sum_ready, 1)
            dve.wait_ge(last_t_done, 1)
            row_statistics(out_norm, rows_of(ps_x_nat), out_stats)
            dve.wait_ge(out_stats, 2 * PAIRS - 1)
            mean_and_variance(out_norm, out_var)
            dve.wait_ge(last_sum_ready, 1)
            state_update(end, STEPS - 1, 1, h0_t[1], last_h_ready)
            dve.wait_ge(out_stored[0], 16 * (PAIRS - 1))
            dve.wait_ge(out_rstd, 2 * PAIRS - 1)
            normalise(out_norm, rows_of(result[0]), rows_of(ps_x_nat), out_ready)
            dve.wait_ge(last_t_done, 2)
            row_statistics(h0_norm, rows_of(by_node(ps_z)), out_stats)
            dve.wait_ge(out_stats, 2 * PAIRS)
            mean_and_variance(h0_norm, out_var)
            dve.wait_ge(out_stored[1], 16 * (PAIRS - 1))
            dve.wait_ge(out_rstd, 2 * PAIRS)
            for half in range(2):
                normalise(h0_norm, rows_of(result[1]), rows_of(by_node(ps_z)), out_ready,
                          range(half * G // 2, (half + 1) * G // 2))

        @block.gpsimd
        def _(pool):
            pool.memset(ident[:, :], 0.0).then_inc(ident_zero, 1)
            pool.memset(minus_half[:, :], -0.5)
            pool.memset(eps[:, :], EPS).then_inc(norm_constants, 1)
            pool.wait_ge(ident_zero, 1)
            pool.affine_select(out=ident[:, :], in_=ident[:, :], compare_op=ALU.not_equal, fill=1.0, base=0,
                               pattern=[[-1, P]], channel_multiplier=1).then_inc(ident_ready, 1)
            pool.wait_ge(norm_constants, 1)

            def add_bias(p, g):
                pool.wait_ge(x_loaded[g], (p + 1) * 16)
                if isinstance(p, int) and p == 0:
                    pool.wait_ge(bias_in_s, 16)
                else:
                    pool.wait_ge(y_added, group_no(p - 1, g) + 1)
                pool.tensor_tensor(x_bias[g][:, :, :], x_in[g][:, :, :],
                                   bias_row[:, :].unsqueeze(1).to_broadcast([P, G, D]), ALU.add).then_inc(x_biased, 1)

            def inverse_deviation(norm, var_ready, eps_added, rstd_ready, p, g):
                _, meanvar, var_eps, rstd = norm
                pool.wait_ge(var_ready, group_no(p, g) + 1)
                pool.tensor_tensor(var_eps[:, :], meanvar[:, :, 1], eps[:, :], ALU.add).then_inc(eps_added, 1)
                pool.wait_ge(eps_added, group_no(p, g) + 1)
                pool.tensor_tensor(rstd[:, :], var_eps[:, :], minus_half[:, :], ALU.pow).then_inc(rstd_ready, 1)

            for g in range(2):
                add_bias(0, g)
            for g in range(2):
                inverse_deviation(h0_norm, h0_var, h0_var_eps, h0_rstd, 0, g)

            def pair(p, first, last):
                if not last:
                    for g in range(2):
                        add_bias(p + 1, g)
                if not first:
                    for g in range(2):
                        inverse_deviation(out_norm, out_var, out_var_eps, out_rstd, p - 1, g)
                if not last:
                    for g in range(2):
                        inverse_deviation(h0_norm, h0_var, h0_var_eps, h0_rstd, p + 1, g)

            run_pairs(pool, pair)
            for g, norm in enumerate((out_norm, h0_norm)):
                inverse_deviation(norm, out_var, out_var_eps, out_rstd, PAIRS - 1, g)


def kernel(x, adj, L0_gnn_weight, L0_gnn_bias, L1_gnn_w3_w, L1_gnn_w3_b, L1_gnn_u3_w, L1_gnn_u3_b, L1_gnn_w4_w,
           L1_gnn_w4_b, L1_gnn_w5_w, L1_gnn_w5_b, L1_gnn_u5_w, L1_gnn_u5_b):
    import numpy as np
    import concourse.bacc as bacc
    from concourse.bass_utils import run_bass_kernel_spmd

    def t(a):
        return np.ascontiguousarray(np.asarray(a).T)

    biases = np.stack([np.asarray(b) for b in (L1_gnn_w3_b, L1_gnn_w4_b, L1_gnn_w5_b, L1_gnn_u3_b, L1_gnn_u5_b)])
    arrays = {
        "x": np.ascontiguousarray(x),
        "adj_t": t(adj),
        "w0": np.ascontiguousarray(L0_gnn_weight),
        "b0": np.ascontiguousarray(L0_gnn_bias).reshape(1, -1),
        "w3_t": t(L1_gnn_w3_w),
        "w4_t": t(L1_gnn_w4_w),
        "w5_t": t(L1_gnn_w5_w),
        "u3_t": t(L1_gnn_u3_w),
        "u5_t": t(L1_gnn_u5_w),
        "biases": np.ascontiguousarray(biases.reshape(5, C, P).transpose(2, 0, 1)),
    }
    nc = bacc.Bacc("TRN2", target_bir_lowering=False, num_devices=1)
    args = [nc.dram_tensor(n, a.shape, mybir.dt.from_np(a.dtype), kind="ExternalInput").ap() for n, a in arrays.items()]
    out = nc.dram_tensor("out", arrays["x"].shape, F32, kind="ExternalOutput").ap()
    gnn_kernel(nc, *args, out)
    r = run_bass_kernel_spmd(nc, [arrays], core_ids=[0])
    return r.results[0]["out"]
```

```python
from contextlib import ExitStack

import concourse.bass as bass
from concourse import mybir

F32 = mybir.dt.float32
F32R = mybir.dt.float32r
ALU = mybir.AluOpType
ACT = mybir.ActivationFunctionType

P = 128
G = 4
C = 2
STEPS = 3
SLOTS = 2 * STEPS
EPS = 1e-5


def gnn_kernel(nc, x, adj_t, w0, b0, w3_t, w4_t, w5_t, u3_t, u5_t, biases, out):
    B, N, D = x.shape
    assert N == P and D == C * P and B % (2 * G) == 0
    PAIRS = B // (2 * G)
    COLS = G * N
    Q = 32
    BLOCKS = P // Q
    MOVED = 16 * BLOCKS

    x_groups = x.rearrange("(n b) m d -> n m b d", b=G)
    out_groups = out.rearrange("(n b) m d -> n m b d", b=G)

    with ExitStack() as ctx:
        def sb(name, shape, dt=F32):
            return ctx.enter_context(nc.sbuf_tensor(name, shape, dt))

        def sem(name):
            return ctx.enter_context(nc.semaphore(name))

        def two(make, name, *args):
            return [make(f"{name}_{g}", *args) for g in "ab"]

        adjt = sb("adjt", [P, N])
        ident = sb("ident", [P, P])
        bias_row = sb("bias_row", [P, D])
        bias_in = sb("bias_in", [P, 5, C])
        bias_z = sb("bias_z", [P, C])
        bias_r = sb("bias_r", [P, C])
        bias_h = sb("bias_h", [P, C])
        minus_half = sb("minus_half", [P, G])
        eps = sb("eps", [P, G])
        w0_raw = sb("w0_raw", [P, C, D])
        w_raw = [sb(f"w{n}_raw", [P, 2 * C, D]) for n in (3, 4, 5)]
        u_raw = [sb(f"u{n}_raw", [P, C, D]) for n in (3, 5)]
        w0_hi, w0_lo = sb("w0_hi", [P, C, D], F32R), sb("w0_lo", [P, C, D], F32R)
        gate_hi = {n: sb(f"{n}_hi", [P, C, D], F32R) for n in ("w3", "w4", "w5", "u3", "u5")}
        gate_lo = {n: sb(f"{n}_lo", [P, C, D], F32R) for n in ("w3", "w4", "w5", "u3", "u5")}

        gate_raw = {"u3": u_raw[0][:, :, :], "u5": u_raw[1][:, :, :],
                    "w3": w_raw[0][:, 0:C, :], "w4": w_raw[1][:, 0:C, :], "w5": w_raw[2][:, 0:C, :]}

        x_in = two(sb, "x_in", [P, G, D])
        x_bias = two(sb, "x_bias", [P, G, D])
        h0_nat = two(sb, "h0_nat", [P, G, D])
        h0_t = two(sb, "h0_t", [P, C, COLS])
        h_t = two(sb, "h_t", [P, C, COLS])
        h_hi, h_lo = two(sb, "h_hi", [P, C, COLS], F32R), two(sb, "h_lo", [P, C, COLS], F32R)
        a_hi, a_lo = two(sb, "a_hi", [P, C, COLS], F32R), two(sb, "a_lo", [P, C, COLS], F32R)
        result = two(sb, "result", [P, G, D])

        h0_blocks = sb("h0_blocks", [P, BLOCKS, G * C, Q])
        h0_moved_in = two(sb, "h0_moved_in", [P, BLOCKS, G * C, Q])
        last_blocks = two(sb, "last_blocks", [P, BLOCKS, C * G, Q])
        last_moved_in = two(sb, "last_moved_in", [P, BLOCKS, C * G, Q])

        h_blocks = sb("h_blocks", [P, C, BLOCKS, G, Q])
        h_moved_in = sb("h_moved_in", [P, C, BLOCKS, G, Q])
        h_nat = sb("h_nat", [P, G, D])
        ax_hi, ax_lo = sb("ax_hi", [P, C, COLS], F32R), sb("ax_lo", [P, C, COLS], F32R)
        u_sb = sb("u_sb", [P, C, COLS])
        z_sb = sb("z_sb", [P, C, COLS])
        rh = sb("rh", [P, C, COLS])
        rh_hi, rh_lo = sb("rh_hi", [P, C, COLS], F32R), sb("rh_lo", [P, C, COLS], F32R)
        hv = sb("hv", [P, C, COLS])

        def scratch(name, elements):
            return nc.dram_tensor(name, [P, BLOCKS, elements], F32, kind="Internal").ap()

        h_scratch = [scratch(f"h_scratch_{c}", G * Q) for c in range(C)]
        h0_scratch, last_scratch = scratch("h0_scratch", C * G * Q), two(scratch, "last_scratch", C * G * Q)

        def norm_buffers(name):
            return (sb(name + "_sums", [P, G, 6]), sb(name + "_meanvar", [P, G, 2]),
                    sb(name + "_var_eps_sb", [P, G]), sb(name + "_rstd_sb", [P, G]))

        h0_norm, out_norm = norm_buffers("h0"), norm_buffers("out")

        ps_r = ctx.enter_context(nc.psum_tensor("ps_r", [P, C, COLS], F32))
        ps_z = ctx.enter_context(nc.psum_tensor("ps_z", [P, C, COLS], F32))
        ps_h = ctx.enter_context(nc.psum_tensor("ps_h", [P, C, COLS], F32))
        ps_x = ctx.enter_context(nc.psum_tensor("ps_x", [P, C, COLS], F32))

        def by_node(ps):
            return ps[:, :, :].rearrange("p c (b d) -> p (c b) d", d=D)

        ps_x_nat = by_node(ps_x)

        adj_in, w0_in, gates_in, bias_in_s = sem("adj_in"), sem("w0_in"), sem("gates_in"), sem("bias_in_s")
        x_loaded = two(sem, "x_loaded")
        out_stored = two(sem, "out_stored")
        h0_written, last_written = two(sem, "h0_written"), two(sem, "last_written")
        h0_moved, last_moved = two(sem, "h0_moved"), two(sem, "last_moved")
        h_written, h_moved = ([sem(f"{n}_{c}") for c in range(C)] for n in ("h_written", "h_moved"))
        ident_zero, ident_ready = sem("ident_zero"), sem("ident_ready")
        w0_hi_ready, w0_ready = sem("w0_hi_ready"), sem("w0_ready")
        gate_sum, gates_hi_ready, gates_ready = sem("gate_sum"), sem("gates_hi_ready"), sem("gates_ready")
        biases_ready = sem("biases_ready")
        norm_constants = sem("norm_constants")
        u_done, z_done, r_done, h_done = sem("u_done"), sem("z_done"), sem("r_done"), sem("h_done")
        graph_done = sem("graph_done")
        first_t_done, last_t_done = sem("first_t_done"), sem("last_t_done")
        ax_done, y_done = sem("ax_done"), sem("y_done")
        u_copied, z_ready, r_ready = sem("u_copied"), sem("z_ready"), sem("r_ready")
        rh_hi_ready, hv_ready, h_hi_ready = sem("rh_hi_ready"), sem("hv_ready"), sem("h_hi_ready")
        a_hi_ready, ax_hi_ready = sem("a_hi_ready"), sem("ax_hi_ready")
        h_nat_ready, h0_t_ready = sem("h_nat_ready"), sem("h0_t_ready")
        z_added, rh_ready, rh_lo_ready = sem("z_added"), sem("rh_ready"), sem("rh_lo_ready")
        diff_ready, scaled_ready = sem("diff_ready"), sem("scaled_ready")
        h_ready, h_lo_ready = sem("h_ready"), sem("h_lo_ready")
        last_h_ready = sem("last_h_ready")
        h_blocks_ready = sem("h_blocks_ready")
        h0_blocks_ready, last_blocks_ready = sem("h0_blocks_ready"), sem("last_blocks_ready")
        a_lo_ready, ax_lo_ready = sem("a_lo_ready"), sem("ax_lo_ready")
        y_added, h0_stats, h0_var, h0_ready = sem("y_added"), sem("h0_stats"), sem("h0_var"), sem("h0_ready")
        out_stats, out_var, out_ready = sem("out_stats"), sem("out_var"), sem("out_ready")
        last_sum_ready = sem("last_sum_ready")
        x_biased = sem("x_biased")
        h0_var_eps, h0_rstd = sem("h0_var_eps"), sem("h0_rstd")
        out_var_eps, out_rstd = sem("out_var_eps"), sem("out_rstd")

        def slot_no(p, k):
            return p * SLOTS + k

        def group_no(p, g):
            return p * 2 + g

        def move_no(p, k):
            return p * (SLOTS - 2) + k

        def run_pairs(eng, pair):
            pair(0, True, PAIRS == 1)
            if PAIRS > 2:
                with eng.Fori(1, PAIRS - 1) as p:
                    pair(p, False, False)
            if PAIRS > 1:
                pair(PAIRS - 1, False, True)

        block = ctx.enter_context(nc.Block())

        @block.sync
        def _(sp):
            sp.dma_start(adjt[:, :], adj_t).then_inc(adj_in, 16)
            sp.dma_start(x_in[0][:, :, :], x_groups[0]).then_inc(x_loaded[0], 16)
            sp.dma_start(w0_raw[:, :, :], w0.rearrange("(c p) o -> p c o", p=P)).then_inc(w0_in, 16)
            sp.dma_start(bias_row[:, :], b0.to_broadcast([P, D])).then_inc(bias_in_s, 16)
            sp.dma_start(x_in[1][:, :, :], x_groups[1]).then_inc(x_loaded[1], 16)
            sp.dma_start(u_raw[0][:, :, :], u3_t.rearrange("(c p) o -> p c o", p=P)).then_inc(gates_in, 16)
            for raw, w in zip(w_raw, (w3_t, w4_t, w5_t)):
                sp.dma_start(raw[:, :, :], w.rearrange("(c p) o -> p c o", p=P)).then_inc(gates_in, 16)
            sp.dma_start(u_raw[1][:, :, :], u5_t.rearrange("(c p) o -> p c o", p=P)).then_inc(gates_in, 16)
            sp.dma_start(bias_in[:, :, :], biases).then_inc(gates_in, 16)

            def to_dram(dst, blocks, written):
                sp.dma_start(dst, blocks).then_inc(written, 16)

            def to_quadrants(moved_in, src, moved):
                by_target = src.rearrange("(i q) j e -> j q i e", q=Q)
                for to in range(BLOCKS):
                    sp.dma_start(moved_in[to * Q:(to + 1) * Q].rearrange("q i m e -> q i (m e)"),
                                 by_target[to]).then_inc(moved, 16)

            def flat(blocks):
                return blocks.rearrange("p j m e -> p j (m e)")

            def move_step(p, k):
                m = move_no(p, k - 1)
                for c in range(C):
                    sp.wait_ge(h_blocks_ready, 2 * m + c + 1)
                    to_dram(h_scratch[c], flat(h_blocks[:, c, :, :, :]), h_written[c])
                for c in range(C):
                    sp.wait_ge(h_written[c], (m + 1) * 16)
                    if not (isinstance(m, int) and m == 0):
                        sp.wait_ge(h_nat_ready, 2 * m)
                    to_quadrants(h_moved_in[:, c, :, :, :], h_scratch[c], h_moved[c])

            def h0_out(p, g):
                sp.wait_ge(h0_blocks_ready, group_no(p - 1, g) + 1)
                to_dram(h0_scratch, flat(h0_blocks[:, :, :, :]), h0_written[g])

            def h0_back(p, g):
                sp.wait_ge(h0_written[g], p * 16)
                sp.wait_ge(h0_t_ready, group_no(p - 1, g) + 1)
                to_quadrants(h0_moved_in[g][:, :, :, :], h0_scratch, h0_moved[g])

            def move_last(p, g):
                sp.wait_ge(last_blocks_ready, group_no(p, g) + 1)
                to_dram(last_scratch[g], flat(last_blocks[g][:, :, :, :]), last_written[g])
                sp.wait_ge(last_written[g], (p + 1) * 16)
                if not (isinstance(p, int) and p == 0):
                    sp.wait_ge(out_ready, group_no(p - 1, g) + 1)
                to_quadrants(last_moved_in[g][:, :, :, :], last_scratch[g], last_moved[g])

            def store(p, g):
                sp.wait_ge(out_ready, group_no(p, g) + 1)
                sp.dma_start(out_groups[group_no(p, g)], result[g][:, :, :]).then_inc(out_stored[g], 16)

            def pair(p, first, last):
                if not last:
                    for g in range(2):
                        sp.wait_ge(ax_done, group_no(p, g) + 1)
                        sp.wait_ge(x_biased, group_no(p, g) + 1)
                        sp.dma_start(x_in[g][:, :, :], x_groups[group_no(p + 1, g)]).then_inc(x_loaded[g], 16)
                if not first:
                    move_last(p - 1, 1)
                move_step(p, 1)
                move_step(p, 2)
                if not first:
                    store(p - 1, 0)
                move_step(p, 3)
                if not last:
                    h0_out(p + 1, 0)
                move_step(p, 4)
                if not first:
                    store(p - 1, 1)
                if not last:
                    h0_back(p + 1, 0)
                    h0_out(p + 1, 1)
                    h0_back(p + 1, 1)
                    move_last(p, 0)

            run_pairs(sp, pair)
            store(PAIRS - 1, 0)
            for half in range(2):
                rows = slice(half * G // 2, (half + 1) * G // 2)
                sp.wait_ge(out_ready, 2 * PAIRS - 1 + half + 1)
                sp.dma_start(out_groups[2 * PAIRS - 1][:, rows, :], result[1][:, rows, :]).then_inc(out_stored[1], 16)
            sp.wait_ge(out_stored[0], 16 * PAIRS)
            sp.wait_ge(out_stored[1], 16 * (PAIRS + 1))

        @block.tensor
        def _(pe):
            def split_product(psum, name, hi, lo, start, stop, signal=None, wait=None, outputs=range(C)):
                w_hi, w_lo = gate_hi[name], gate_lo[name]
                for o in outputs:
                    for n, (w, v) in enumerate(((w_hi, hi), (w_lo, hi), (w_hi, lo))):
                        for c in range(C):
                            if wait is not None and o == 0:
                                wait(n, c)
                            ends = n == 2 and c == C - 1
                            mm = pe.matmul(psum[:, o, :], w[:, c, o * P:(o + 1) * P], v[:, c, :],
                                           start=start and n == 0 and c == 0, stop=stop and ends,
                                           skip_group_check=True)
                    if signal is not None:
                        mm.then_inc(signal, 1)

            def graph(psum, nat, signal):
                for c in range(C):
                    for b in range(G):
                        mm = pe.matmul(psum[:, c, b * N:(b + 1) * N], nat[:, b, c * P:(c + 1) * P], adjt[:, :],
                                       start=True, stop=True)
                mm.then_inc(signal, 1)

            def to_nodes(psum, src, signal, chunk_wait=None):
                for c in range(C):
                    if chunk_wait is not None:
                        chunk_wait(c)
                    for b in range(G):
                        mm = pe.transpose(by_node(psum)[:, b, c * P:(c + 1) * P], src[:, c, b * N:(b + 1) * N],
                                          ident[:, :])
                mm.then_inc(signal, 1)

            def to_features(psum, src, signal):
                for c in range(C):
                    for b in range(G):
                        mm = pe.transpose(psum[:, c, b * N:(b + 1) * N], src[:, b, c * P:(c + 1) * P], ident[:, :])
                mm.then_inc(signal, 1)

            def first_graph(psum, p, g):
                pe.wait_ge(x_loaded[g], (p + 1) * 16)
                graph(psum, x_in[g], ax_done)

            def first_weights(psum, hi, lo, p, g):
                pe.wait_ge(ax_lo_ready, group_no(p, g) + 1)
                for b in range(G):
                    for c in range(C):
                        cols = slice(b * N, (b + 1) * N)
                        for n, (v, w) in enumerate(((hi, w0_hi), (hi, w0_lo), (lo, w0_hi))):
                            mm = pe.matmul(by_node(psum)[:, b, :], v[:, c, cols], w[:, c, :],
                                           start=n == 0 and c == 0, stop=n == 2 and c == C - 1,
                                           skip_group_check=True)
                mm.then_inc(y_done, 1)

            pe.wait_ge(adj_in, 16)
            first_graph(ps_x, 0, 0)
            first_graph(ps_z, 0, 1)
            pe.wait_ge(w0_ready, 1)
            first_weights(ps_r, ax_hi, ax_lo, 0, 0)
            first_weights(ps_h, a_hi[1], a_lo[1], 0, 1)
            pe.wait_ge(ident_ready, 1)
            pe.wait_ge(h0_ready, 1)
            to_features(ps_z, h0_nat[0], first_t_done)
            graph(ps_x, h0_nat[0], graph_done)

            def slot(p, k, first, last):
                s, g = divmod(k, 2)
                i = slot_no(p, k)
                begin = first and k == 0
                other = 1 - g
                pe.wait_ge(h_lo_ready, i + 1)
                if not begin:
                    pe.wait_ge(r_ready, 2 * i)
                if begin:
                    pe.wait_ge(gates_ready, 1)
                split_product(ps_r, "u3", h_hi[g], h_lo[g], True, True, u_done)

                if begin:
                    pe.wait_ge(h0_ready, 2)
                    pe.wait_ge(a_lo_ready, 1)
                    to_features(ps_x, h0_nat[1], first_t_done)

                def a_parts(n, c):
                    if n == 0:
                        pe.wait_ge(a_hi_ready, i + 1)
                    if n == 2:
                        pe.wait_ge(a_lo_ready, i + 1)

                if not begin:
                    pe.wait_ge(z_added, i)
                if begin:
                    pe.wait_ge(gates_ready, 2)
                split_product(ps_z, "w3", a_hi[g], a_lo[g], True, True, z_done, a_parts)

                if not last and k in (1, 3):
                    first_graph(ps_x, p + 1, k // 2)
                if not last and k in (2, 4):
                    first_weights(ps_x, ax_hi, ax_lo, p + 1, k // 2 - 1)

                pe.wait_ge(u_copied, i + 1)
                if begin:
                    pe.wait_ge(gates_ready, 3)
                split_product(ps_r, "w4", a_hi[g], a_lo[g], False, True, r_done)

                if last and k == SLOTS - 1:
                    pe.wait_ge(last_h_ready, 2 * PAIRS - 1)
                    to_nodes(ps_x, h_t[0], last_t_done)

                if not begin:
                    pe.wait_ge(hv_ready, 2 * i)
                if begin:
                    pe.wait_ge(gates_ready, 4)
                split_product(ps_h, "w5", a_hi[g], a_lo[g], True, False)

                def rh_parts(n, c):
                    if n == 0:
                        pe.wait_ge(rh_hi_ready, 2 * i + c + 1)
                    if n == 2:
                        pe.wait_ge(rh_lo_ready, 2 * i + c + 1)

                if begin:
                    pe.wait_ge(gates_ready, 5)
                split_product(ps_h, "u5", rh_hi, rh_lo, False, True, h_done, rh_parts, range(0, 1))

                if 1 <= k <= SLOTS - 2:
                    pe.wait_ge(h_nat_ready, 2 * (move_no(p, k - 1) + 1))
                    if not last and k in (1, 3):
                        pe.wait_ge(ax_lo_ready, group_no(p + 1, k // 2) + 1)
                    elif not last:
                        pe.wait_ge(y_added, group_no(p + 1, k // 2 - 1) + 1)
                    graph(ps_x, h_nat, graph_done)
                elif not (last and k == SLOTS - 1):
                    if begin:
                        pe.wait_ge(h0_t_ready, 2)
                    pe.wait_ge(h0_ready, group_no(p if k == 0 else p + 1, other) + 1)
                    graph(ps_x, h0_nat[other], graph_done)

                split_product(ps_h, "u5", rh_hi, rh_lo, False, True, h_done, None, range(1, C))

            def pair(p, first, last):
                for k in range(SLOTS):
                    slot(p, k, first, last)

            run_pairs(pe, pair)

            def last_state_there(c):
                pe.wait_ge(last_h_ready, 2 * PAIRS - 1 + c + 1)

            to_nodes(ps_z, h_t[1], last_t_done, last_state_there)

        @block.scalar
        def _(act):
            def copy(dst, src):
                return act.activation(dst, src, ACT.Copy)

            act.wait_ge(w0_in, 16)
            copy(w0_hi[:, :, :], w0_raw[:, :, :]).then_inc(w0_hi_ready, 1)

            def first_graph_parts(psum, hi, p, g):
                act.wait_ge(ax_done, group_no(p, g) + 1)
                copy(hi[:, :, :], psum[:, :, :]).then_inc(ax_hi_ready, 1)

            def first_state(p, g):
                if isinstance(p, int) and p == 0:
                    act.wait_ge(first_t_done, g + 1)
                    copy(h0_t[g][:, :, :], (ps_z, ps_x)[g][:, :, :]).then_inc(h0_t_ready, 1)
                else:
                    act.wait_ge(h0_moved[g], p * MOVED)
                    for c in range(C):
                        cp = copy(h0_t[g][:, c, :].rearrange("p (b i e) -> p b i e", b=G, e=Q),
                                  h0_moved_in[g][:, :, :, :].rearrange("p i (b c) e -> p c b i e", c=C)[:, c])
                    cp.then_inc(h0_t_ready, 1)

            def first_state_part(p, g):
                act.wait_ge(h0_t_ready, group_no(p, g) + 1)
                copy(h_hi[g][:, :, :], h0_t[g][:, :, :]).then_inc(h_hi_ready, 1)

            def graph_parts(i, g):
                act.wait_ge(graph_done, i + 1)
                copy(a_hi[g][:, :, :], ps_x[:, :, :]).then_inc(a_hi_ready, 1)

            def candidate(i, c):
                act.wait_ge(h_done, 2 * i + c + 1)
                act.activation(hv[:, c, :], ps_h[:, c, :], ACT.Tanh, bias=bias_h[:, c:c + 1]).then_inc(hv_ready, 1)

            first_graph_parts(ps_x, ax_hi, 0, 0)
            first_graph_parts(ps_z, a_hi[1], 0, 1)
            act.wait_ge(gate_sum, 3)
            for n, name in enumerate(("u3", "w3", "w4", "w5", "u5")):
                copy(gate_hi[name][:, :, :], gate_raw[name]).then_inc(gates_hi_ready, 1)
            first_state(0, 0)
            first_state_part(0, 0)
            graph_parts(0, 0)

            def slot(p, k, first, last):
                s, g = divmod(k, 2)
                i = slot_no(p, k)
                begin = first and k == 0
                other = 1 - g
                if begin:
                    act.wait_ge(biases_ready, 1)
                act.wait_ge(u_done, 2 * i + 2)
                copy(u_sb[:, :, :], ps_r[:, :, :]).then_inc(u_copied, 1)
                if 1 <= k <= SLOTS - 2:
                    act.wait_ge(h_ready, 2 * i)
                    copy(h_hi[other][:, :, :], h_t[other][:, :, :]).then_inc(h_hi_ready, 1)
                if k == 0:
                    if not begin:
                        act.wait_ge(last_h_ready, group_no(p - 1, 1) + 1)
                    first_state(p, 1)
                if k == SLOTS - 1 and not last:
                    act.wait_ge(last_h_ready, group_no(p, 0) + 1)
                    first_state(p + 1, 0)
                if not last and k in (1, 3):
                    first_graph_parts(ps_x, ax_hi, p + 1, k // 2)
                for c in range(C):
                    act.wait_ge(r_done, 2 * i + c + 1)
                    r = act.activation(rh[:, c, :], ps_r[:, c, :], ACT.Sigmoid, bias=bias_r[:, c:c + 1])
                    r.then_inc(r_ready, 1)
                for c in range(C):
                    act.wait_ge(rh_ready, 2 * i + c + 1)
                    copy(rh_hi[:, c, :], rh[:, c, :]).then_inc(rh_hi_ready, 1)
                if k == 0:
                    first_state_part(p, 1)
                if k == SLOTS - 1 and not last:
                    first_state_part(p + 1, 0)
                if 1 <= k <= SLOTS - 2:
                    m = move_no(p, k - 1)
                    act.wait_ge(graph_done, i + 1)
                    for c in range(C):
                        act.wait_ge(h_moved[c], (m + 1) * MOVED)
                        copy(h_nat[:, :, c * P:(c + 1) * P].rearrange("p b (i e) -> p b i e", e=Q),
                             h_moved_in[:, c, :, :, :].rearrange("p i b e -> p b i e")).then_inc(h_nat_ready, 1)
                act.wait_ge(z_added, i + 1)
                for c in range(C):
                    z = act.activation(z_sb[:, c, :], z_sb[:, c, :], ACT.Sigmoid, bias=bias_z[:, c:c + 1])
                z.then_inc(z_ready, 1)
                candidate(i, 0)
                if not (last and k == SLOTS - 1):
                    graph_parts(i + 1, other)
                candidate(i, 1)

            def pair(p, first, last):
                for k in range(SLOTS):
                    slot(p, k, first, last)

            run_pairs(act, pair)

        @block.vector
        def _(dve):
            def low_part(dst, full, hi):
                return dve.tensor_tensor(dst, full, hi.bitcast(F32), ALU.subtract)

            def first_graph_parts(psum, hi, lo, p, g):
                dve.wait_ge(ax_hi_ready, group_no(p, g) + 1)
                low_part(lo[:, :, :], psum[:, :, :], hi[:, :, :]).then_inc(ax_lo_ready, 1)

            def row_statistics(norm, rows, measured):
                sums = norm[0]
                for b in range(G):
                    st = dve.bn_stats(sums[:, b, :], rows(b))
                st.then_inc(measured, 1)

            def mean_and_variance(norm, ready):
                sums, meanvar = norm[0], norm[1]
                for b in range(G):
                    mv = dve.bn_aggr(meanvar[:, b, :], sums[:, b, :])
                mv.then_inc(ready, 1)

            def normalise(norm, dst, rows, ready, batches=range(G)):
                meanvar, rstd = norm[1], norm[3]
                for b in batches:
                    ts = dve.tensor_scalar(dst(b), rows(b), meanvar[:, b, 0:1], rstd[:, b:b + 1],
                                           ALU.subtract, ALU.mult)
                ts.then_inc(ready, 1)

            def rows_of(tensor):
                return lambda b: tensor[:, b, :]

            def first_sum(psum, p, g):
                dve.wait_ge(y_done, group_no(p, g) + 1)
                dve.wait_ge(x_biased, group_no(p, g) + 1)
                dve.tensor_tensor(h0_nat[g][:, :, :], by_node(psum), x_bias[g][:, :, :], ALU.add).then_inc(y_added, 1)

            def first_statistics(p, g):
                dve.wait_ge(y_added, group_no(p, g) + 1)
                row_statistics(h0_norm, rows_of(h0_nat[g]), h0_stats)

            def first_norm(p, g):
                dve.wait_ge(h0_rstd, group_no(p, g) + 1)
                normalise(h0_norm, rows_of(h0_nat[g]), rows_of(h0_nat[g]), h0_ready)

            def first_blocks(p, g):
                if g == 1:
                    dve.wait_ge(h0_moved[0], p * MOVED)
                elif not (isinstance(p, int) and p == 1):
                    dve.wait_ge(h0_moved[1], (p - 1) * MOVED)
                dve.wait_ge(h0_ready, group_no(p, g) + 1)
                dve.transpose(h0_blocks[:, :, :, :].rearrange("p j m e -> p m j e"),
                              h0_nat[g][:, :, :].rearrange("p b (c j e) -> p (b c) j e", c=C, e=Q)
                              ).then_inc(h0_blocks_ready, 1)

            def last_state_blocks(p, g):
                if not (isinstance(p, int) and p == 0):
                    dve.wait_ge(last_moved[g], p * MOVED)
                dve.wait_ge(last_h_ready, group_no(p, g) + 1)
                dve.transpose(last_blocks[g][:, :, :, :].rearrange("p j m e -> p m j e"),
                              h_t[g][:, :, :].rearrange("p c (b j e) -> p (c b) j e", b=G, e=Q)
                              ).then_inc(last_blocks_ready, 1)

            def last_rows(g):
                return lambda b: last_moved_in[g][:, :, :, :].rearrange("p i (c b) e -> p b c i e", b=G)[:, b]

            def result_rows(g):
                return lambda b: result[g][:, b, :].rearrange("p (c i e) -> p c i e", c=C, e=Q)

            def result_statistics(p, g):
                dve.wait_ge(last_moved[g], (p + 1) * MOVED)
                row_statistics(out_norm, last_rows(g), out_stats)

            def result_norm(p, g):
                if not (isinstance(p, int) and p == 0):
                    dve.wait_ge(out_stored[g], p * 16)
                dve.wait_ge(out_rstd, group_no(p, g) + 1)
                normalise(out_norm, result_rows(g), last_rows(g), out_ready)

            def first_state_parts(i, p, g):
                dve.wait_ge(h_hi_ready, i + 1)
                dve.wait_ge(h0_t_ready, group_no(p, g) + 1)
                low_part(h_lo[g][:, :, :], h0_t[g][:, :, :], h_hi[g][:, :, :]).then_inc(h_lo_ready, 1)

            def graph_parts(i, g):
                dve.wait_ge(a_hi_ready, i + 1)
                low_part(a_lo[g][:, :, :], ps_x[:, :, :], a_hi[g][:, :, :]).then_inc(a_lo_ready, 1)

            def state_update(i, s, g, c, added=None, ready=h_ready):
                before = h0_t[g] if s == 0 else h_t[g]
                added = before if added is None else added
                dve.wait_ge(hv_ready, 2 * i + c + 1)
                dve.tensor_tensor(hv[:, c, :], hv[:, c, :], before[:, c, :], ALU.subtract).then_inc(diff_ready, 1)
                dve.wait_ge(diff_ready, 2 * i + c + 1)
                if c == 0:
                    dve.wait_ge(z_ready, i + 1)
                dve.tensor_tensor(hv[:, c, :], hv[:, c, :], z_sb[:, c, :], ALU.mult).then_inc(scaled_ready, 1)
                dve.wait_ge(scaled_ready, 2 * i + c + 1)
                dve.tensor_tensor(h_t[g][:, c, :], hv[:, c, :], added[:, c, :], ALU.add).then_inc(ready, 1)

            def state_blocks(i, m, g, c):
                if not (isinstance(m, int) and m == 0):
                    dve.wait_ge(h_moved[c], m * MOVED)
                dve.wait_ge(h_ready, 2 * i + c + 1)
                dve.transpose(h_blocks[:, c, :, :, :].rearrange("p j b e -> p b j e"),
                              h_t[g][:, c, :].rearrange("p (b j e) -> p b j e", b=G, e=Q)
                              ).then_inc(h_blocks_ready, 1)

            def add_residual(i, g):
                dve.wait_ge(h_ready, 2 * i + 2)
                dve.tensor_tensor(h_t[g][:, :, :], h_t[g][:, :, :], h0_t[g][:, :, :], ALU.add).then_inc(last_h_ready, 1)

            dve.wait_ge(w0_hi_ready, 1)
            low_part(w0_lo[:, :, :], w0_raw[:, :, :], w0_hi[:, :, :]).then_inc(w0_ready, 1)
            first_graph_parts(ps_x, ax_hi, ax_lo, 0, 0)
            first_graph_parts(ps_z, a_hi[1], a_lo[1], 0, 1)
            first_sum(ps_r, 0, 0)
            first_statistics(0, 0)
            dve.wait_ge(h0_stats, 1)
            mean_and_variance(h0_norm, h0_var)
            dve.wait_ge(gates_in, 16 * 6)
            for raw in w_raw:
                dve.tensor_tensor(raw[:, 0:C, :], raw[:, 0:C, :], raw[:, C:2 * C, :], ALU.add).then_inc(gate_sum, 1)
            dve.tensor_tensor(bias_z[:, :], bias_in[:, 0, :], bias_in[:, 3, :], ALU.add)
            dve.tensor_tensor(bias_r[:, :], bias_in[:, 1, :], bias_in[:, 3, :], ALU.add)
            dve.tensor_tensor(bias_h[:, :], bias_in[:, 2, :], bias_in[:, 4, :], ALU.add).then_inc(biases_ready, 1)
            first_norm(0, 0)
            first_sum(ps_h, 0, 1)
            first_statistics(0, 1)
            dve.wait_ge(h0_stats, 2)
            mean_and_variance(h0_norm, h0_var)

            def gate_low_part(n, name):
                dve.wait_ge(gates_hi_ready, n + 1)
                low_part(gate_lo[name][:, :, :], gate_raw[name], gate_hi[name][:, :, :]).then_inc(gates_ready, 1)

            gate_low_part(0, "u3")
            first_state_parts(0, 0, 0)
            gate_low_part(1, "w3")
            graph_parts(0, 0)
            gate_low_part(2, "w4")
            first_norm(0, 1)
            gate_low_part(3, "w5")
            gate_low_part(4, "u5")

            def slot(p, k, first, last):
                s, g = divmod(k, 2)
                i = slot_no(p, k)
                begin = first and k == 0
                other = 1 - g
                if k == 0 and not begin:
                    add_residual(i - 1, 1)
                if k == SLOTS - 1:
                    add_residual(i - 1, 0)
                if k in (2, 4) and not first:
                    result_norm(p - 1, k // 2 - 1)
                if not last and k in (3, 5):
                    first_norm(p + 1, k // 2 - 1)
                dve.wait_ge(u_copied, i + 1)
                dve.wait_ge(z_done, 2 * i + 2)
                dve.tensor_tensor(z_sb[:, :, :], ps_z[:, :, :], u_sb[:, :, :], ALU.add).then_inc(z_added, 1)
                if k == 0 and not begin:
                    last_state_blocks(p - 1, 1)
                if not last and k in (1, 3):
                    first_graph_parts(ps_x, ax_hi, ax_lo, p + 1, k // 2)
                if not last and k in (2, 4):
                    first_sum(ps_x, p + 1, k // 2 - 1)
                before = h0_t[g] if s == 0 else h_t[g]
                for c in range(C):
                    dve.wait_ge(r_ready, 2 * i + c + 1)
                    dve.tensor_tensor(rh[:, c, :], rh[:, c, :], before[:, c, :], ALU.mult).then_inc(rh_ready, 1)
                for c in range(C):
                    dve.wait_ge(rh_hi_ready, 2 * i + c + 1)
                    low_part(rh_lo[:, c, :], rh[:, c, :], rh_hi[:, c, :]).then_inc(rh_lo_ready, 1)
                if 1 <= k <= SLOTS - 2:
                    dve.wait_ge(h_hi_ready, i + 2)
                    low_part(h_lo[other][:, :, :], h_t[other][:, :, :], h_hi[other][:, :, :]).then_inc(h_lo_ready, 1)
                if k == 0:
                    first_state_parts(i + 1, p, 1)
                if k == SLOTS - 1 and not last:
                    first_state_parts(i + 1, p + 1, 0)
                if not last and k in (3, 5):
                    first_blocks(p + 1, k // 2 - 1)
                if not last and k in (2, 4):
                    first_statistics(p + 1, k // 2 - 1)
                    dve.wait_ge(h0_stats, group_no(p + 1, k // 2 - 1) + 1)
                if k == SLOTS - 1 and not last:
                    last_state_blocks(p, 0)
                if k in (1, 3) and not first:
                    result_statistics(p - 1, k // 2)
                    dve.wait_ge(out_stats, group_no(p - 1, k // 2) + 1)
                if last and k == SLOTS - 1:
                    return
                state_update(i, s, g, 0)
                if k in (1, 3) and not first:
                    mean_and_variance(out_norm, out_var)
                if not last and k in (2, 4):
                    mean_and_variance(h0_norm, h0_var)
                graph_parts(i + 1, other)
                if k < SLOTS - 2:
                    state_blocks(i, move_no(p, k), g, 0)
                state_update(i, s, g, 1)
                if k < SLOTS - 2:
                    state_blocks(i, move_no(p, k), g, 1)

            def pair(p, first, last):
                for k in range(SLOTS):
                    slot(p, k, first, last)

            run_pairs(dve, pair)
            end = slot_no(PAIRS - 1, SLOTS - 1)
            dve.tensor_tensor(h0_t[1][:, :, :], h0_t[1][:, :, :], h_t[1][:, :, :], ALU.add).then_inc(last_sum_ready, 1)
            dve.wait_ge(last_t_done, 1)
            row_statistics(out_norm, rows_of(ps_x_nat), out_stats)
            dve.wait_ge(out_stats, 2 * PAIRS - 1)
            mean_and_variance(out_norm, out_var)
            dve.wait_ge(last_sum_ready, 1)
            for c in range(C):
                state_update(end, STEPS - 1, 1, c, h0_t[1], last_h_ready)
            dve.wait_ge(last_t_done, 2)
            row_statistics(h0_norm, rows_of(by_node(ps_z)), out_stats)
            dve.wait_ge(out_stats, 2 * PAIRS)
            mean_and_variance(h0_norm, out_var)
            dve.wait_ge(out_stored[0], 16 * (PAIRS - 1))
            dve.wait_ge(out_rstd, 2 * PAIRS - 1)
            normalise(out_norm, rows_of(result[0]), rows_of(ps_x_nat), out_ready)
            dve.wait_ge(out_stored[1], 16 * (PAIRS - 1))
            dve.wait_ge(out_rstd, 2 * PAIRS)
            for half in range(2):
                normalise(h0_norm, rows_of(result[1]), rows_of(by_node(ps_z)), out_ready,
                          range(half * G // 2, (half + 1) * G // 2))

        @block.gpsimd
        def _(pool):
            pool.memset(ident[:, :], 0.0).then_inc(ident_zero, 1)
            pool.memset(minus_half[:, :], -0.5)
            pool.memset(eps[:, :], EPS).then_inc(norm_constants, 1)
            pool.wait_ge(ident_zero, 1)
            pool.affine_select(out=ident[:, :], in_=ident[:, :], compare_op=ALU.not_equal, fill=1.0, base=0,
                               pattern=[[-1, P]], channel_multiplier=1).then_inc(ident_ready, 1)
            pool.wait_ge(norm_constants, 1)

            def add_bias(p, g):
                pool.wait_ge(x_loaded[g], (p + 1) * 16)
                if isinstance(p, int) and p == 0:
                    pool.wait_ge(bias_in_s, 16)
                else:
                    pool.wait_ge(y_added, group_no(p - 1, g) + 1)
                pool.tensor_tensor(x_bias[g][:, :, :], x_in[g][:, :, :],
                                   bias_row[:, :].unsqueeze(1).to_broadcast([P, G, D]), ALU.add).then_inc(x_biased, 1)

            def inverse_deviation(norm, var_ready, eps_added, rstd_ready, p, g):
                _, meanvar, var_eps, rstd = norm
                pool.wait_ge(var_ready, group_no(p, g) + 1)
                pool.tensor_tensor(var_eps[:, :], meanvar[:, :, 1], eps[:, :], ALU.add).then_inc(eps_added, 1)
                pool.wait_ge(eps_added, group_no(p, g) + 1)
                pool.tensor_tensor(rstd[:, :], var_eps[:, :], minus_half[:, :], ALU.pow).then_inc(rstd_ready, 1)

            for g in range(2):
                add_bias(0, g)
            for g in range(2):
                inverse_deviation(h0_norm, h0_var, h0_var_eps, h0_rstd, 0, g)

            def pair(p, first, last):
                if not last:
                    for g in range(2):
                        add_bias(p + 1, g)
                for g in range(2):
                    if not first:
                        inverse_deviation(out_norm, out_var, out_var_eps, out_rstd, p - 1, g)
                    if not last:
                        inverse_deviation(h0_norm, h0_var, h0_var_eps, h0_rstd, p + 1, g)

            run_pairs(pool, pair)
            for g, norm in enumerate((out_norm, h0_norm)):
                inverse_deviation(norm, out_var, out_var_eps, out_rstd, PAIRS - 1, g)


def kernel(x, adj, L0_gnn_weight, L0_gnn_bias, L1_gnn_w3_w, L1_gnn_w3_b, L1_gnn_u3_w, L1_gnn_u3_b, L1_gnn_w4_w,
           L1_gnn_w4_b, L1_gnn_w5_w, L1_gnn_w5_b, L1_gnn_u5_w, L1_gnn_u5_b):
    import numpy as np
    import concourse.bacc as bacc
    from concourse.bass_utils import run_bass_kernel_spmd

    def t(a):
        return np.ascontiguousarray(np.asarray(a).T)

    biases = np.stack([np.asarray(b) for b in (L1_gnn_w3_b, L1_gnn_w4_b, L1_gnn_w5_b, L1_gnn_u3_b, L1_gnn_u5_b)])
    arrays = {
        "x": np.ascontiguousarray(x),
        "adj_t": t(adj),
        "w0": np.ascontiguousarray(L0_gnn_weight),
        "b0": np.ascontiguousarray(L0_gnn_bias).reshape(1, -1),
        "w3_t": t(L1_gnn_w3_w),
        "w4_t": t(L1_gnn_w4_w),
        "w5_t": t(L1_gnn_w5_w),
        "u3_t": t(L1_gnn_u3_w),
        "u5_t": t(L1_gnn_u5_w),
        "biases": np.ascontiguousarray(biases.reshape(5, C, P).transpose(2, 0, 1)),
    }
    nc = bacc.Bacc("TRN2", target_bir_lowering=False, num_devices=1)
    args = [nc.dram_tensor(n, a.shape, mybir.dt.from_np(a.dtype), kind="ExternalInput").ap() for n, a in arrays.items()]
    out = nc.dram_tensor("out", arrays["x"].shape, F32, kind="ExternalOutput").ap()
    gnn_kernel(nc, *args, out)
    r = run_bass_kernel_spmd(nc, [arrays], core_ids=[0])
    return r.results[0]["out"]
```
